# Optimizing a Trainium2 kernel written in Bass

```python
import numpy as np
import jax
import jax.numpy as jnp

def _softmax(x, axis=-1):
    return jax.nn.softmax(x, axis=axis)

def _gelu(x):
    return jax.nn.gelu(x, approximate=True)

def _silu(x):
    return jax.nn.silu(x)

def _sigmoid(x):
    return jax.nn.sigmoid(x)

def _layernorm(x, axis=-1, eps=1e-05):
    m = jnp.mean(x, axis=axis, keepdims=True)
    v = jnp.var(x, axis=axis, keepdims=True)
    return (x - m) / jnp.sqrt(v + eps)

def _scatter_add(tgt, idx, src, axis=0):
    return tgt.at[idx].add(src)

def _segment_sum(src, seg, n):
    return jax.ops.segment_sum(src, seg, n)
kernel_name = 'mk_seq_postln_d2_jaxref_r8_5112fa'

def setup_inputs(seed: int=0):
    np.random.seed(seed)
    _w = jnp.asarray

    def _L0_attn_setup():
        import jax, jax.numpy as jnp
        import numpy as np
        import math
        D_MODEL = 256
        N_HEADS = 16
        D_HEAD = 128
        BATCH = 2
        SEQ = 256
        key = jax.random.key(seed)
        ks = jax.random.split(key, 5)
        std = 0.02
        x = jax.random.normal(ks[0], (BATCH, SEQ, D_MODEL), dtype=jnp.float32)
        W_Q = std * jax.random.normal(ks[1], (N_HEADS, D_HEAD, D_MODEL), dtype=jnp.float32)
        W_K = std * jax.random.normal(ks[2], (N_HEADS, D_HEAD, D_MODEL), dtype=jnp.float32)
        W_V = std * jax.random.normal(ks[3], (N_HEADS, D_HEAD, D_MODEL), dtype=jnp.float32)
        W_O = std * jax.random.normal(ks[4], (N_HEADS, D_MODEL, D_HEAD), dtype=jnp.float32)
        return {'x': x, 'W_Q': W_Q, 'W_K': W_K, 'W_V': W_V, 'W_O': W_O}
    _L0_attn_in = _L0_attn_setup()

    def _L0_ffn_setup():
        import jax, jax.numpy as jnp
        import numpy as np
        B, S, H = (2, 128, 256)
        E, K = (8, 2)
        I = 176
        IS = 704
        WSCALE = 0.02
        key = jax.random.key(seed)
        ks = jax.random.split(key, 9)
        f32 = jnp.float32
        return {'hidden_states': jax.random.normal(ks[0], (B, S, H), dtype=f32), 'gate_w': jax.random.normal(ks[1], (E, H), dtype=f32) * WSCALE, 'w_gate': jax.random.normal(ks[2], (E, H, I), dtype=f32) * WSCALE, 'w_up': jax.random.normal(ks[3], (E, H, I), dtype=f32) * WSCALE, 'w_down': jax.random.normal(ks[4], (E, I, H), dtype=f32) * WSCALE, 'sw_gate': jax.random.normal(ks[5], (H, IS), dtype=f32) * WSCALE, 'sw_up': jax.random.normal(ks[6], (H, IS), dtype=f32) * WSCALE, 'sw_down': jax.random.normal(ks[7], (IS, H), dtype=f32) * WSCALE, 'shared_gate_w': jax.random.normal(ks[8], (H, 1), dtype=f32) * WSCALE}
    _L0_ffn_in = _L0_ffn_setup()

    def _L1_attn_setup():
        import jax, jax.numpy as jnp
        import numpy as np
        B, S, D = (2, 256, 256)
        H, G = (16, 4)
        HD = D // H
        KV = HD * G
        key = jax.random.key(seed)
        ks = jax.random.split(key, 5)
        scale = 1.0 / np.sqrt(D)
        return {'x': jax.random.normal(ks[0], (B, S, D), dtype=jnp.float32), 'Wqkv': jax.random.normal(ks[1], (D, D + 2 * KV), dtype=jnp.float32) * scale, 'bqkv': jax.random.normal(ks[2], (D + 2 * KV,), dtype=jnp.float32) * 0.01, 'Wout': jax.random.normal(ks[3], (D, D), dtype=jnp.float32) * scale, 'bout': jax.random.normal(ks[4], (D,), dtype=jnp.float32) * 0.01}
    _L1_attn_in = _L1_attn_setup()

    def _L1_ffn_setup():
        import jax, jax.numpy as jnp
        import numpy as np
        E = 16
        D = 256
        H = 176
        HS = 2 * 176
        TOP_K = 6
        ROUTE_SCALE = 1.0
        key = jax.random.key(seed)
        ks = jax.random.split(key, 16)
        s = 0.02
        return {'x': jax.random.normal(ks[0], (4, 128, D), dtype=jnp.float32), 'gate_w': jax.random.normal(ks[1], (E, D), dtype=jnp.float32) * s, 'gate_b': jax.random.normal(ks[2], (E,), dtype=jnp.float32) * s, 'w1': jax.random.normal(ks[3], (E, H, D), dtype=jnp.float32) * s, 'b1': jax.random.normal(ks[4], (E, H), dtype=jnp.float32) * s, 'w2': jax.random.normal(ks[5], (E, D, H), dtype=jnp.float32) * s, 'b2': jax.random.normal(ks[6], (E, D), dtype=jnp.float32) * s, 'w3': jax.random.normal(ks[7], (E, H, D), dtype=jnp.float32) * s, 'b3': jax.random.normal(ks[8], (E, H), dtype=jnp.float32) * s, 'ws1': jax.random.normal(ks[9], (HS, D), dtype=jnp.float32) * s, 'bs1': jax.random.normal(ks[10], (HS,), dtype=jnp.float32) * s, 'ws2': jax.random.normal(ks[11], (D, HS), dtype=jnp.float32) * s, 'bs2': jax.random.normal(ks[12], (D,), dtype=jnp.float32) * s, 'ws3': jax.random.normal(ks[13], (HS, D), dtype=jnp.float32) * s, 'bs3': jax.random.normal(ks[14], (HS,), dtype=jnp.float32) * s}
    _L1_ffn_in = _L1_ffn_setup()
    _d = {'L0_attn_x': _L0_attn_in['x'], 'L0_attn_W_Q': _L0_attn_in['W_Q'], 'L0_attn_W_K': _L0_attn_in['W_K'], 'L0_attn_W_V': _L0_attn_in['W_V'], 'L0_attn_W_O': _L0_attn_in['W_O'], 'L0_ffn_gate_w': _L0_ffn_in['gate_w'], 'L0_ffn_w_gate': _L0_ffn_in['w_gate'], 'L0_ffn_w_up': _L0_ffn_in['w_up'], 'L0_ffn_w_down': _L0_ffn_in['w_down'], 'L0_ffn_sw_gate': _L0_ffn_in['sw_gate'], 'L0_ffn_sw_up': _L0_ffn_in['sw_up'], 'L0_ffn_sw_down': _L0_ffn_in['sw_down'], 'L0_ffn_shared_gate_w': _L0_ffn_in['shared_gate_w'], 'L1_attn_Wqkv': _L1_attn_in['Wqkv'], 'L1_attn_bqkv': _L1_attn_in['bqkv'], 'L1_attn_Wout': _L1_attn_in['Wout'], 'L1_attn_bout': _L1_attn_in['bout'], 'L1_ffn_gate_w': _L1_ffn_in['gate_w'], 'L1_ffn_gate_b': _L1_ffn_in['gate_b'], 'L1_ffn_w1': _L1_ffn_in['w1'], 'L1_ffn_b1': _L1_ffn_in['b1'], 'L1_ffn_w2': _L1_ffn_in['w2'], 'L1_ffn_b2': _L1_ffn_in['b2'], 'L1_ffn_w3': _L1_ffn_in['w3'], 'L1_ffn_b3': _L1_ffn_in['b3'], 'L1_ffn_ws1': _L1_ffn_in['ws1'], 'L1_ffn_bs1': _L1_ffn_in['bs1'], 'L1_ffn_ws2': _L1_ffn_in['ws2'], 'L1_ffn_bs2': _L1_ffn_in['bs2'], 'L1_ffn_ws3': _L1_ffn_in['ws3'], 'L1_ffn_bs3': _L1_ffn_in['bs3']}
    _x0 = _d['L0_attn_x']
    _d['L0_attn_x'] = jax.random.normal(jax.random.fold_in(jax.random.key(seed), 1), (2, 1024, 256), dtype=_x0.dtype)
    del _x0
    return _d

def reference(L0_attn_x, L0_attn_W_Q, L0_attn_W_K, L0_attn_W_V, L0_attn_W_O, L0_ffn_gate_w, L0_ffn_w_gate, L0_ffn_w_up, L0_ffn_w_down, L0_ffn_sw_gate, L0_ffn_sw_up, L0_ffn_sw_down, L0_ffn_shared_gate_w, L1_attn_Wqkv, L1_attn_bqkv, L1_attn_Wout, L1_attn_bout, L1_ffn_gate_w, L1_ffn_gate_b, L1_ffn_w1, L1_ffn_b1, L1_ffn_w2, L1_ffn_b2, L1_ffn_w3, L1_ffn_b3, L1_ffn_ws1, L1_ffn_bs1, L1_ffn_ws2, L1_ffn_bs2, L1_ffn_ws3, L1_ffn_bs3):

    def _L0_attn_ref(x, W_Q, W_K, W_V, W_O):
        import jax, jax.numpy as jnp
        import numpy as np
        import math
        D_MODEL = 256
        N_HEADS = 16
        D_HEAD = 128
        BATCH = 2
        SEQ = 256
        d_head = W_Q.shape[1]
        seq_len = x.shape[1]
        scale = 1.0 / math.sqrt(d_head)
        q = jnp.einsum('bsd,hed->bhse', x, W_Q)
        k = jnp.einsum('bsd,hed->bhse', x, W_K)
        v = jnp.einsum('bsd,hed->bhse', x, W_V)
        scores = jnp.einsum('bhse,bhme->bhsm', q, k) * scale
        causal = jnp.triu(jnp.ones((seq_len, seq_len), dtype=bool), k=1)
        scores = jnp.where(causal, jnp.float32(-1000000000.0), scores)
        pattern = jax.nn.softmax(scores, axis=-1)
        z = jnp.einsum('bhsm,bhme->bhse', pattern, v)
        out = jnp.einsum('bhse,hde->bsd', z, W_O)
        return out

    def _L0_ffn_ref(hidden_states, gate_w, w_gate, w_up, w_down, sw_gate, sw_up, sw_down, shared_gate_w):
        import jax, jax.numpy as jnp
        import numpy as np
        B, S, H = (2, 128, 256)
        E, K = (8, 2)
        I = 176
        IS = 704
        WSCALE = 0.02
        x = hidden_states
        logits = jnp.einsum('bsh,eh->bse', x, gate_w)
        probs = jax.nn.softmax(logits, axis=-1)
        top_w, top_i = jax.lax.top_k(probs, K)
        top_w = top_w / jnp.sum(top_w, axis=-1, keepdims=True)
        onehot = jax.nn.one_hot(top_i, E, dtype=x.dtype)
        combine = jnp.einsum('bsk,bske->bse', top_w, onehot)
        g = jnp.einsum('bsh,ehi->besi', x, w_gate)
        u = jnp.einsum('bsh,ehi->besi', x, w_up)
        h = jax.nn.silu(g) * u
        expert_out = jnp.einsum('besi,eih->besh', h, w_down)
        moe_out = jnp.einsum('besh,bse->bsh', expert_out, combine)
        sh = jax.nn.silu(x @ sw_gate) * (x @ sw_up)
        shared_out = sh @ sw_down
        shared_gate = jax.nn.sigmoid(x @ shared_gate_w)
        return moe_out + shared_out * shared_gate

    def _L1_attn_ref(x, Wqkv, bqkv, Wout, bout):
        import jax, jax.numpy as jnp
        import numpy as np
        B, S, D = (2, 256, 256)
        H, G = (16, 4)
        HD = D // H
        KV = HD * G
        b, s, _ = x.shape
        qkv = x @ Wqkv + bqkv
        q, k, v = jnp.split(qkv, [D, D + KV], axis=-1)
        q = q.reshape(b, s, H, HD)
        k = jnp.tile(k.reshape(b, s, G, HD), (1, 1, H // G, 1))
        v = jnp.tile(v.reshape(b, s, G, HD), (1, 1, H // G, 1))
        scores = jnp.einsum('bqhd,bkhd->bhqk', q, k) / HD
        prob = jax.nn.softmax(scores, axis=-1)
        out = jnp.einsum('bhqk,bkhd->bqhd', prob, v).reshape(b, s, D)
        return out @ Wout + bout

    def _L1_ffn_ref(x, gate_w, gate_b, w1, b1, w2, b2, w3, b3, ws1, bs1, ws2, bs2, ws3, bs3):
        import jax, jax.numpy as jnp
        import numpy as np
        E = 16
        D = 256
        H = 176
        HS = 2 * 176
        TOP_K = 6
        ROUTE_SCALE = 1.0
        shape = x.shape
        xf = x.reshape(-1, shape[-1])
        scores = xf @ gate_w.T
        probs = jax.nn.softmax(scores.astype(jnp.float32), axis=-1)
        biased = probs + gate_b
        _, idx = jax.lax.top_k(biased, TOP_K)
        weights = jnp.take_along_axis(probs, idx, axis=1) * ROUTE_SCALE
        weights = weights.astype(x.dtype)
        onehot = jax.nn.one_hot(idx, E, dtype=weights.dtype)
        cw = jnp.einsum('tk,tke->te', weights, onehot)

        def expert_step(y, params):
            W1, B1, W2, B2, W3, B3, c = params
            h = jax.nn.silu(xf @ W1.T + B1) * (xf @ W3.T + B3)
            out = h @ W2.T + B2
            return (y + c[:, None] * out, None)
        y0 = jnp.zeros_like(xf)
        y, _ = jax.lax.scan(expert_step, y0, (w1, b1, w2, b2, w3, b3, cw.T))
        z = jax.nn.silu(xf @ ws1.T + bs1) * (xf @ ws3.T + bs3) @ ws2.T + bs2
        return (y + z).reshape(shape)
    x = L0_attn_x
    x = _layernorm(x + _L0_attn_ref(x, L0_attn_W_Q, L0_attn_W_K, L0_attn_W_V, L0_attn_W_O), axis=-1)
    x = _layernorm(x + _L0_ffn_ref(x, L0_ffn_gate_w, L0_ffn_w_gate, L0_ffn_w_up, L0_ffn_w_down, L0_ffn_sw_gate, L0_ffn_sw_up, L0_ffn_sw_down, L0_ffn_shared_gate_w), axis=-1)
    x = _layernorm(x + _L1_attn_ref(x, L1_attn_Wqkv, L1_attn_bqkv, L1_attn_Wout, L1_attn_bout), axis=-1)
    x = _layernorm(x + _L1_ffn_ref(x, L1_ffn_gate_w, L1_ffn_gate_b, L1_ffn_w1, L1_ffn_b1, L1_ffn_w2, L1_ffn_b2, L1_ffn_w3, L1_ffn_b3, L1_ffn_ws1, L1_ffn_bs1, L1_ffn_ws2, L1_ffn_bs2, L1_ffn_ws3, L1_ffn_bs3), axis=-1)
    return x

_drawn_inputs = setup_inputs


def setup_inputs(seed=0):
    import zlib

    import numpy as np

    out = dict(_drawn_inputs(seed))
    spreads = {}
    factors = {'L0_attn_W_Q': 8.0,
     'L0_attn_W_K': 8.0,
     'L0_ffn_gate_w': 6.551,
     'L0_ffn_w_gate': 5.747,
     'L0_ffn_w_up': 5.697,
     'L0_ffn_w_down': 5.684,
     'L0_ffn_sw_gate': 4.034,
     'L0_ffn_sw_up': 3.999,
     'L0_ffn_sw_down': 4.001,
     'L0_ffn_shared_gate_w': 8.0,
     'L1_attn_bqkv': 5.888,
     'L1_attn_bout': 5.832,
     'L1_ffn_gate_w': 8.0,
     'L1_ffn_gate_b': 8.0,
     'L1_ffn_w1': 8.0,
     'L1_ffn_b1': 8.0,
     'L1_ffn_w2': 8.0,
     'L1_ffn_b2': 26.581,
     'L1_ffn_w3': 8.0,
     'L1_ffn_b3': 8.0,
     'L1_ffn_ws1': 2.864,
     'L1_ffn_bs1': 23.377,
     'L1_ffn_ws2': 2.811,
     'L1_ffn_bs2': 14.491,
     'L1_ffn_ws3': 2.832,
     'L1_ffn_bs3': 26.055}
    for name, (base, spread) in spreads.items():
        noise = np.random.default_rng([zlib.crc32(name.encode()), seed]).standard_normal(out[name].shape)
        drawn = base * np.exp(spread * noise) if base else spread * noise
        out[name] = jnp.asarray(drawn.astype(out[name].dtype))
    for name, factor in factors.items():
        out[name] = (out[name] * factor).astype(out[name].dtype)
    return out
```

```python
from contextlib import ExitStack

import numpy as np

import concourse.bass as bass
from concourse import mybir

F32 = mybir.dt.float32
F32R = mybir.dt.float32r
ACT = mybir.ActivationFunctionType
ALU = mybir.AluOpType
AX = mybir.AxisListType

P = 128
B, S, D = 2, 1024, 256
T = B * S
DT = D // P
NTOK = T // P
CH = 512
EPS = 1e-5

H0, E0 = 16, 128
H1, HD1, G1 = 16, 16, 4
KV1 = HD1 * G1

NE = 8
INTER = 176
SLICE = P // NE
NJ = INTER // SLICE
HS0, HS1 = 704, 352
NSH0, NSH1 = -(-HS0 // P), -(-HS1 // P)


class Phase:

    def __init__(self, nc, tag, psum=None):
        self.nc, self.tag, self.stack, self.psum, self.bank = nc, tag, ExitStack(), psum, 0

    def __enter__(self):
        return self

    def __exit__(self, *a):
        self.stack.close()

    def sb(self, name, shape, dt=F32):
        return self.stack.enter_context(self.nc.sbuf_tensor(f"{self.tag}_{name}", shape, dt))

    def ps(self, shape):
        size = int(np.prod(shape[1:]))
        banks = size // CH
        b0, self.bank = self.bank, self.bank + banks
        assert size == banks * CH and self.bank <= 8
        flat = self.psum[0:shape[0], b0:b0 + banks, :].rearrange("p b n -> p (b n)")
        names = " ".join(f"d{k}" for k in range(len(shape) - 1))
        return flat.rearrange(f"p ({names}) -> p {names}", **{f"d{k}": n for k, n in enumerate(shape[1:])})

    def sem(self, name):
        return self.stack.enter_context(self.nc.semaphore(f"{self.tag}_{name}"))

    def block(self):
        return self.stack.enter_context(self.nc.Block())


def mm3(pe, out, a_hi, a_lo, b_hi, b_lo, first, last):
    pe.matmul(out, a_hi, b_hi, start=first, stop=False)
    pe.matmul(out, a_hi, b_lo, start=False, stop=False)
    return pe.matmul(out, a_lo, b_hi, start=False, stop=last)


def layer_norm_semaphores(nc, stack):
    names = ("eps_set", "y_turned", "stats_done", "mv_done", "std_done", "rstd_done", "xn_done", "x_turned",
             "hi_done", "lo_done", "stored0", "stored1")
    return {name: stack.enter_context(nc.semaphore(f"norm_{name}")) for name in names}


def layer_norm(nc, tag, nth, sems, yT, xh, xl, ident, psum, out=None):
    Q = 4
    NG = NTOK // Q
    with Phase(nc, tag, psum) as ph:
        tok = ph.ps([P, 2, Q, D])
        back = ph.ps([P, 2, DT, Q * P])
        stats = ph.sb("stats", [P, Q, 6])
        mv = ph.sb("mv", [P, Q, 2])
        std = ph.sb("std", [P, Q])
        rstd = ph.sb("rstd", [P, Q])
        eps = ph.sb("eps", [P, 1])
        xn = ph.sb("xn", [P, 2, Q, D])
        eps_set, y_turned, stats_done, mv_done = (sems[n] for n in ("eps_set", "y_turned", "stats_done", "mv_done"))
        std_done, rstd_done, xn_done = (sems[n] for n in ("std_done", "rstd_done", "xn_done"))
        x_turned, hi_done, lo_done = (sems[n] for n in ("x_turned", "hi_done", "lo_done"))
        stored = [sems["stored0"], sems["stored1"]]
        G0, T0, D0 = nth * NG, nth * NTOK, nth * NG * DT
        block = ph.block()

        @block.tensor
        def _(pe):
            def turn_y(g):
                if g >= 2:
                    pe.wait_ge(xn_done, T0 + Q * (g - 1))
                for q in range(Q):
                    for dt in range(DT):
                        t0 = (g * Q + q) * P
                        m = pe.transpose(tok[:, g % 2, q, dt * P:(dt + 1) * P], yT[:, dt, t0:t0 + P], ident[:])
                    m.then_inc(y_turned, 1)

            def turn_x(g):
                if g >= 2:
                    pe.wait_ge(lo_done, D0 + DT * (g - 1))
                for q in range(Q):
                    pe.wait_ge(xn_done, T0 + g * Q + q + 1)
                    for dt in range(DT):
                        m = pe.transpose(back[:, g % 2, dt, q * P:(q + 1) * P],
                                         xn[:, g % 2, q, dt * P:(dt + 1) * P], ident[:])
                m.then_inc(x_turned, 1)

            turn_y(0)
            for g in range(NG):
                if g + 1 < NG:
                    turn_y(g + 1)
                if out is None:
                    turn_x(g)

        @block.vector
        def _(dve):
            dve.memset(eps[:], EPS).then_inc(eps_set, 1)

            def take_stats(g):
                dve.wait_ge(y_turned, T0 + Q * (g + 1))
                if g >= 1:
                    dve.wait_ge(mv_done, T0 + Q * g)
                    dve.wait_ge(xn_done, T0 + Q * g)
                for q in range(Q):
                    dve.bn_stats(stats[:, q, :], tok[:, g % 2, q, :]).then_inc(stats_done, 1)
                for q in range(Q):
                    dve.wait_ge(stats_done, T0 + g * Q + q + 1)
                    dve.bn_aggr(mv[:, q, :], stats[:, q, :]).then_inc(mv_done, 1)

            def normalise(g):
                dve.wait_ge(std_done, G0 + g + 1)
                dve.reciprocal(rstd[:], std[:]).then_inc(rstd_done, 1)
                dve.wait_ge(rstd_done, G0 + g + 1)
                if g >= 2:
                    if out is None:
                        dve.wait_ge(x_turned, G0 + g - 1)
                    else:
                        dve.wait_ge(stored[g % 2], 16 * (g // 2))
                for q in range(Q):
                    dve.tensor_scalar(xn[:, g % 2, q, :], tok[:, g % 2, q, :], mv[:, q, 0:1], rstd[:, q:q + 1],
                                      ALU.subtract, ALU.mult).then_inc(xn_done, 1)

            def keep_lo(g):
                for dt in range(DT):
                    dve.wait_ge(hi_done, D0 + g * DT + dt + 1)
                    t0 = g * Q * P
                    dve.tensor_tensor(xl[:, dt, t0:t0 + Q * P], back[:, g % 2, dt, :], xh[:, dt, t0:t0 + Q * P].bitcast(F32),
                                      ALU.subtract).then_inc(lo_done, 1)

            for g in range(NG):
                take_stats(g)
                if out is None and g >= 1:
                    keep_lo(g - 1)
                normalise(g)
            if out is None:
                keep_lo(NG - 1)

        @block.scalar
        def _(act):
            def root(g):
                act.wait_ge(mv_done, T0 + Q * (g + 1))
                if g >= 1:
                    act.wait_ge(rstd_done, G0 + g)
                act.activation(std[:], mv[:, :, 1], ACT.Sqrt, bias=eps[:, 0:1]).then_inc(std_done, 1)

            act.wait_ge(eps_set, nth + 1)
            for g in range(NG):
                root(g)
                if out is None:
                    act.wait_ge(x_turned, G0 + g + 1)
                    t0 = g * Q * P
                    for dt in range(DT):
                        act.activation(xh[:, dt, t0:t0 + Q * P], back[:, g % 2, dt, :], ACT.Copy).then_inc(hi_done, 1)

        if out is not None:
            @block.sync
            def _(sp):
                rows = out.rearrange("(g q p) d -> g p q d", q=Q, p=P)
                for g in range(NG):
                    sp.wait_ge(xn_done, T0 + Q * (g + 1))
                    sp.dma_start(rows[g], xn[:, g % 2, :, :]).then_inc(stored[g % 2], 16)
                for s in range(2):
                    sp.wait_ge(stored[s], 16 * (NG // 2))


def mixture(nc, tag, w, xh, xl, yT, ident, psum, shared_gate):
    groups = w["groups"]
    ne = NE * groups
    nr = ne + (2 if shared_gate else 0)
    nsh = w["shared_tiles"]
    topk = w["topk"]
    biased = w["gate_b"] is not None
    nmap = groups + (1 if shared_gate else 0)
    NT = groups * NJ + nsh
    unmapped = 0 if shared_gate else nsh
    HALF = T // 2
    NC = HALF // CH

    with Phase(nc, tag, psum) as ph:
        cmap = ph.sb("cmap", [P, nmap, T])
        cT = ph.sb("cT", [ne + 1, T])

        with Phase(nc, tag + "r", psum) as rt:
            gw = rt.sb("gw", [P, DT, nr])
            gwh = rt.sb("gwh", [P, DT, nr], F32R)
            gwl = rt.sb("gwl", [P, DT, nr], F32R)
            sel = rt.sb("sel", [ne + 1, nmap, P])
            gb = rt.sb("gb", [P, ne])
            lg_bank = rt.ps([P, CH])
            lg_ps = lg_bank[:, 0:NTOK * nr].rearrange("p (t n) -> p t n", n=nr)
            turn_ps = rt.ps([ne + 1, 2, CH])
            map_ps = rt.ps([P, 2, CH])
            lg = rt.sb("lg", [P, NTOK, nr])
            mx = rt.sb("mx", [P, NTOK])
            sh = rt.sb("sh", [P, NTOK, ne])
            ex = rt.sb("ex", [P, NTOK, ne])
            sg = rt.sb("sg", [P, NTOK])
            sm = rt.sb("sm", [P, NTOK])
            pr = rt.sb("pr", [P, NTOK, ne])
            bi = rt.sb("bi", [P, NTOK, ne])
            top = rt.sb("top", [P, NTOK, 8])
            rest = rt.sb("rest", [P, NTOK, ne])
            cw = rt.sb("cw", [P, NTOK, ne + 1])
            loaded = rt.sem("loaded")
            hi_done = rt.sem("hi_done")
            lo_done = rt.sem("lo_done")
            logits_done = rt.sem("logits_done")
            shifted = rt.sem("shifted")
            exp_done = rt.sem("exp_done")
            step = rt.sem("step")
            weights_done = rt.sem("weights_done")
            turned = rt.sem("turned")
            cT_done = rt.sem("cT_done")
            mapped = rt.sem("mapped")
            kept = rt.sem("kept")
            block = rt.block()

            @block.sync
            def _(sp):
                sp.dma_start(gw[:], w["gate_w"]).then_inc(loaded, 16)
                sp.dma_start(sel[:], w["sel"]).then_inc(loaded, 16)
                if biased:
                    sp.dma_start(gb[:], w["gate_b"]).then_inc(loaded, 16)

            @block.scalar
            def _(act):
                act.wait_ge(loaded, 48 if biased else 32)
                act.activation(gwh[:], gw[:], ACT.Copy).then_inc(hi_done, 1)
                act.wait_ge(shifted, 1)
                act.activation(ex[:], sh[:], ACT.Exp).then_inc(exp_done, 1)
                if shared_gate:
                    act.activation(sg[:], lg[:, :, ne], ACT.Exp, scale=-1.0).then_inc(exp_done, 1)
                for c in range(T // CH):
                    for m in range(nmap):
                        act.wait_ge(mapped, c * nmap + m + 1)
                        act.activation(cmap[:, m, c * CH:(c + 1) * CH], map_ps[:, (c * nmap + m) % 2, :],
                                       ACT.Copy).then_inc(kept, 1)

            @block.vector
            def _(dve):
                n = [0]

                def chain(i):
                    i.then_inc(step, 1)
                    n[0] += 1
                    dve.wait_ge(step, n[0])

                def spread(a, width):
                    return a[:].unsqueeze(2).to_broadcast([P, NTOK, width])

                dve.wait_ge(loaded, 48 if biased else 32)
                dve.wait_ge(hi_done, 1)
                dve.tensor_tensor(gwl[:], gw[:], gwh[:].bitcast(F32), ALU.subtract).then_inc(lo_done, 1)
                dve.wait_ge(logits_done, 1)
                chain(dve.tensor_copy(lg[:], lg_ps))
                chain(dve.tensor_reduce(mx[:], lg[:, :, 0:ne], AX.X, ALU.max))
                dve.tensor_tensor(sh[:], lg[:, :, 0:ne], spread(mx, ne), ALU.subtract).then_inc(shifted, 1)
                dve.wait_ge(exp_done, 1)
                chain(dve.tensor_reduce(sm[:], ex[:], AX.X, ALU.add))
                chain(dve.reciprocal(sm[:], sm[:]))
                chain(dve.tensor_tensor(pr[:], ex[:], spread(sm, ne), ALU.mult))
                if biased:
                    chain(dve.tensor_tensor(bi[:], pr[:], gb[:].unsqueeze(1).to_broadcast([P, NTOK, ne]), ALU.add))
                else:
                    chain(dve.tensor_copy(bi[:], pr[:]))
                for t in range(NTOK):
                    i = dve.max(top[:, t, :], bi[:, t, :])
                chain(i)
                chain(dve.memset(top[:, :, topk:8], 3.0e38))
                for t in range(NTOK):
                    i = dve.match_replace(rest[:, t, :], top[:, t, :], bi[:, t, :], -3.0e38)
                chain(i)
                chain(dve.tensor_tensor(rest[:], rest[:], bi[:], ALU.not_equal))
                if shared_gate:
                    chain(dve.tensor_tensor(pr[:], pr[:], rest[:], ALU.mult))
                    chain(dve.tensor_reduce(sm[:], pr[:], AX.X, ALU.add))
                    chain(dve.reciprocal(sm[:], sm[:]))
                    chain(dve.tensor_tensor(cw[:, :, 0:ne], pr[:], spread(sm, ne), ALU.mult))
                    dve.wait_ge(exp_done, 2)
                    chain(dve.tensor_scalar(sg[:], sg[:], 1.0, None, ALU.add))
                    dve.reciprocal(cw[:, :, ne], sg[:]).then_inc(weights_done, 1)
                else:
                    chain(dve.memset(cw[:, :, ne:ne + 1], 1.0))
                    dve.tensor_tensor(cw[:, :, 0:ne], pr[:], rest[:], ALU.mult).then_inc(weights_done, 1)
                for c in range(T // CH):
                    dve.wait_ge(turned, c + 1)
                    dve.tensor_copy(cT[:, c * CH:(c + 1) * CH], turn_ps[:, c % 2, :]).then_inc(cT_done, 1)

            @block.tensor
            def _(pe):
                pe.wait_ge(lo_done, 1)
                for t in range(NTOK):
                    for dt in range(DT):
                        i = mm3(pe, lg_ps[:, t, :], xh[:, dt, t * P:(t + 1) * P], xl[:, dt, t * P:(t + 1) * P],
                                gwh[:, dt, :], gwl[:, dt, :], dt == 0, dt == DT - 1)
                i.then_inc(logits_done, 1)
                pe.wait_ge(weights_done, 1)
                for c in range(T // CH):
                    if c >= 2:
                        pe.wait_ge(cT_done, c - 1)
                    for q in range(CH // P):
                        i = pe.transpose(turn_ps[:, c % 2, q * P:(q + 1) * P], cw[:, c * (CH // P) + q, :], ident[:])
                    i.then_inc(turned, 1)
                for c in range(T // CH):
                    pe.wait_ge(cT_done, c + 1)
                    for m in range(nmap):
                        k = c * nmap + m
                        if k >= 2:
                            pe.wait_ge(kept, k - 1)
                        pe.matmul(map_ps[:, k % 2, :], sel[:, m, :], cT[:, c * CH:(c + 1) * CH],
                                  start=True, stop=True).then_inc(mapped, 1)

        raw_gu = ph.sb("raw_gu", [P, 2, 2 * DT * P + 2])
        hi_gu = ph.sb("hi_gu", [P, 2, 2 * DT * P], F32R)
        lo_gu = ph.sb("lo_gu", [P, 2, 2 * DT * P], F32R)
        raw_dn = ph.sb("raw_dn", [P, 2, D])
        hi_dn = ph.sb("hi_dn", [P, 2, D], F32R)
        lo_dn = ph.sb("lo_dn", [P, 2, D], F32R)
        act_s = ph.sb("act_s", [P, NC, CH])
        hid = ph.sb("hid", [P, NC, CH])
        hid2 = ph.sb("hid2", [P, NC, CH])
        hh = ph.sb("hh", [P, 2, NC, CH], F32R)
        hl = ph.sb("hl", [P, 2, NC, CH], F32R)
        idr = ph.sb("idr", [P, P], F32R)
        b2 = ph.sb("b2", [ne + 1, D]) if biased else None
        gate_ps = ph.ps([P, NC, CH])
        up_ps = ph.ps([P, NC, CH])
        y_ps = ph.ps([P, DT, NC, CH])
        raw_gu_in = [ph.sem(f"raw_gu_in{s}") for s in range(2)]
        raw_dn_in = [ph.sem(f"raw_dn_in{s}") for s in range(2)]
        hi_gu_done = ph.sem("hi_gu_done")
        hi_dn_done = ph.sem("hi_dn_done")
        lo_gu_done = ph.sem("lo_gu_done")
        lo_dn_done = ph.sem("lo_dn_done")
        idr_done = ph.sem("idr_done")
        b2_in = ph.sem("b2_in")
        gu_done = ph.sem("gu_done")
        down_done = ph.sem("down_done")
        silu_done = ph.sem("silu_done")
        prod_done = ph.sem("prod_done")
        hid_done = ph.sem("hid_done")
        hhi_done = ph.sem("hhi_done")
        hlo_done = ph.sem("hlo_done")
        y_init = ph.sem("y_init")
        y_kept = ph.sem("y_kept")
        block = ph.block()

        segments = [(g * NJ, NJ, g) for g in range(groups)] + [(groups * NJ, nsh, groups if shared_gate else None)]

        def walk(eng, one, begin=None, end=None):
            for half in range(2):
                if begin:
                    begin(half)
                for first, count, m in segments:
                    k0 = half * NT + first
                    peel = count if first == groups * NJ else 3 if count % 2 else 2
                    for i in range(peel):
                        one(k0 + i, (k0 + i) % 2, m, half)
                    if count > peel:
                        with eng.Fori(0, (count - peel) // 2) as it:
                            k1 = it * 2 + (k0 + peel)
                            one(k1, (k0 + peel) % 2, m, half)
                            one(k1 + 1, (k0 + peel + 1) % 2, m, half)
                if end:
                    end(half)

        def known(k, least):
            return not isinstance(k, int) or k >= least

        def load_count(k, slot):
            return 16 * (k // 2 + 1) if isinstance(k, int) else (k + (2 - slot)) * 8

        def tile_of(k, half):
            return k - half * NT

        @block.sync
        def _(sp):
            if biased:
                sp.dma_start(b2[:], w["b2"]).then_inc(b2_in, 16)

            def one(k, slot, m, half):
                if known(k, 2):
                    sp.wait_ge(prod_done, NC * (k - 1))
                    sp.wait_ge(lo_gu_done, k - 1)
                sp.dma_start(raw_gu[:, slot, :], w["gu"][bass.ds(tile_of(k, half), 1), :, :].rearrange("a p n -> p (a n)")).then_inc(raw_gu_in[slot], 16)
                if known(k, 2):
                    sp.wait_ge(lo_dn_done, k - 1)
                sp.dma_start(raw_dn[:, slot, :], w["down"][bass.ds(tile_of(k, half), 1), :, :].rearrange("a p n -> p (a n)")).then_inc(raw_dn_in[slot], 16)

            walk(sp, one)

        @block.gpsimd
        def _(pool):
            def one(k, slot, m, half):
                pool.wait_ge(hi_gu_done, k + 1)
                pool.tensor_tensor(lo_gu[:, slot, :], raw_gu[:, slot, 0:2 * DT * P], hi_gu[:, slot, :].bitcast(F32),
                                   ALU.subtract).then_inc(lo_gu_done, 1)
                pool.wait_ge(hi_dn_done, k + 1)
                pool.tensor_tensor(lo_dn[:, slot, :], raw_dn[:, slot, :], hi_dn[:, slot, :].bitcast(F32),
                                   ALU.subtract).then_inc(lo_dn_done, 1)

            walk(pool, one)

        @block.tensor
        def _(pe):
            def begin(half):
                if half == 0:
                    pe.wait_ge(idr_done, 1)
                    if biased:
                        pe.wait_ge(b2_in, 16)
                else:
                    pe.wait_ge(y_kept, DT * NC)
                for dt in range(DT):
                    for c in range(NC):
                        t0 = half * HALF + c * CH
                        pe.matmul(y_ps[:, dt, c, :], idr[:], xh[:, dt, t0:t0 + CH], start=True, stop=False)
                        pe.matmul(y_ps[:, dt, c, :], idr[:], xl[:, dt, t0:t0 + CH], start=False, stop=False)
                        if biased:
                            pe.matmul(y_ps[:, dt, c, :], b2[:, dt * P:(dt + 1) * P], cT[:, t0:t0 + CH],
                                      start=False, stop=False)

            def down(k, slot, last):
                pe.wait_ge(hlo_done, NC * k + NC)
                pe.wait_ge(lo_dn_done, k + 1)
                for c in range(NC):
                    for dt in range(DT):
                        d0 = dt * P
                        i = mm3(pe, y_ps[:, dt, c, :], hi_dn[:, slot, d0:d0 + P], lo_dn[:, slot, d0:d0 + P],
                                hh[:, slot, c, :], hl[:, slot, c, :], False, last)
                i.then_inc(down_done, 1)

            def one(k, slot, m, half):
                pe.wait_ge(lo_gu_done, k + 1)
                for c in range(NC):
                    t0 = half * HALF + c * CH
                    if known(k, 1):
                        pe.wait_ge(silu_done, NC * (k - 1) + c + 1)
                        pe.wait_ge(prod_done, NC * (k - 1) + c + 1)
                    for side, dst in enumerate((gate_ps, up_ps)):
                        for dt in range(DT):
                            w0 = (side * DT + dt) * P
                            i = mm3(pe, dst[:, c, :], hi_gu[:, slot, w0:w0 + P], lo_gu[:, slot, w0:w0 + P],
                                    xh[:, dt, t0:t0 + CH], xl[:, dt, t0:t0 + CH], dt == 0, dt == DT - 1)
                    i.then_inc(gu_done, 1)
                if not isinstance(k, int) or k % NT > 0:
                    down(k - 1, 1 - slot, False)

            walk(pe, one, begin, lambda half: down((half + 1) * NT - 1, ((half + 1) * NT - 1) % 2, True))

        @block.scalar
        def _(act):
            act.activation(idr[:], ident[:], ACT.Copy).then_inc(idr_done, 1)

            def round_gu(k, slot):
                act.wait_ge(raw_gu_in[slot], load_count(k, slot))
                if known(k, 2):
                    act.wait_ge(gu_done, NC * (k - 1))
                act.activation(hi_gu[:, slot, :], raw_gu[:, slot, 0:2 * DT * P], ACT.Copy).then_inc(hi_gu_done, 1)

            def round_dn(k, slot):
                act.wait_ge(raw_dn_in[slot], load_count(k, slot))
                if known(k, 2):
                    act.wait_ge(down_done, k - 1)
                act.activation(hi_dn[:, slot, :], raw_dn[:, slot, :], ACT.Copy).then_inc(hi_dn_done, 1)

            round_gu(0, 0)

            def one(k, slot, m, half):
                for c in range(NC):
                    act.wait_ge(gu_done, NC * k + c + 1)
                    if known(k, 1):
                        act.wait_ge(prod_done, NC * (k - 1) + c + 1)
                    act.activation(act_s[:, c, :], gate_ps[:, c, :], ACT.Silu,
                                   bias=raw_gu[:, slot, 2 * DT * P:2 * DT * P + 1]).then_inc(silu_done, 1)
                round_dn(k, slot)
                for c in range(NC):
                    if m is None:
                        act.wait_ge(prod_done, NC * k + c + 1)
                    else:
                        act.wait_ge(hid_done, NC * (k - half * unmapped) + c + 1)
                    if known(k, 2) and c == 0:
                        act.wait_ge(down_done, k - 1)
                    act.activation(hh[:, slot, c, :], (hid if m is None else hid2)[:, c, :], ACT.Copy).then_inc(hhi_done, 1)
                if not isinstance(k, int) or k < 2 * NT - 1:
                    round_gu(k + 1, 1 - slot)

            def end(half):
                act.wait_ge(down_done, (half + 1) * NT)
                for dt in range(DT):
                    for c in range(NC):
                        t0 = half * HALF + c * CH
                        act.activation(yT[:, dt, t0:t0 + CH], y_ps[:, dt, c, :], ACT.Copy).then_inc(y_kept, 1)

            walk(act, one, None, end)

        @block.vector
        def _(dve):
            def one(k, slot, m, half):
                for c in range(NC):
                    t0 = half * HALF + c * CH
                    dve.wait_ge(silu_done, NC * k + c + 1)
                    if known(k, 1):
                        dve.wait_ge(hlo_done, NC * (k - 1) + c + 1)
                    i = dve.scalar_tensor_tensor(out=hid[:, c, :], in0=up_ps[:, c, :],
                                                 scalar=raw_gu[:, slot, 2 * DT * P + 1:2 * DT * P + 2],
                                                 in1=act_s[:, c, :], op0=ALU.add, op1=ALU.mult)
                    i.then_inc(prod_done, 1)
                    dve.wait_ge(prod_done, NC * k + c + 1)
                    if m is not None:
                        dve.tensor_tensor(hid2[:, c, :], hid[:, c, :], cmap[:, m, t0:t0 + CH], ALU.mult).then_inc(hid_done, 1)
                for c in range(NC):
                    dve.wait_ge(hhi_done, NC * k + c + 1)
                    dve.tensor_tensor(hl[:, slot, c, :], (hid if m is None else hid2)[:, c, :], hh[:, slot, c, :].bitcast(F32),
                                      ALU.subtract).then_inc(hlo_done, 1)

            walk(dve, one)


def grouped_attention(nc, tag, a, xh, xl, yT, ident, psum):
    ROWS = 3 * HD1
    MROW = 64
    NCH = S // CH
    NQ = CH // P
    NK = S // P
    NP = NK // 2
    QUADS = H1 // G1
    NU = QUADS * NCH
    ORDER = ("s01", "v0s1")
    W = KV1 // G1 * 2

    with Phase(nc, tag, psum) as ph:
        qd = [nc.dram_tensor(f"{tag}_qd{s}", (D, T), F32, kind="Internal").ap() for s in range(2)]
        ks = ph.sb("ks", [P, B, G1, S], F32R)
        vs = ph.sb("vs", [P, NTOK, G1, W])
        z = ph.sb("z", [P, NTOK, D])

        with Phase(nc, tag + "p", psum) as pj:
            wr = pj.sb("wr", [P, DT, 3 * P])
            wh = pj.sb("wh", [P, DT, 3 * P], F32R)
            wl = pj.sb("wl", [P, DT, 3 * P], F32R)
            bias = pj.sb("bias", [P, 3])
            hi = pj.sb("hi", [P, 3, T], F32R)
            lo = pj.sb("lo", [P, 3, T], F32R)
            kv = pj.sb("kv", [P, T])
            proj_ps = pj.ps([P, 4, CH])
            v_ps = pj.ps([P, 2, CH])
            w_in = pj.sem("w_in")
            wh_done = pj.sem("wh_done")
            wl_done = pj.sem("wl_done")
            cleared = pj.sem("cleared")
            proj_done = pj.sem("proj_done")
            hi_done = pj.sem("hi_done")
            lo_done = pj.sem("lo_done")
            kv_done = pj.sem("kv_done")
            v_turned = pj.sem("v_turned")
            v_kept = pj.sem("v_kept")
            q_out = pj.sem("q_out")
            k_in = pj.sem("k_in")
            NCT = T // CH
            block = pj.block()

            @block.sync
            def _(sp):
                sp.dma_start(wr[:], a["wqkv1"]).then_inc(w_in, 16)
                sp.dma_start(bias[:], a["bqkv1"]).then_inc(w_in, 16)
                sp.wait_ge(lo_done, NCT)
                sp.wait_ge(cleared, 3)
                for b in range(B):
                    for g in range(G1):
                        for r, src in enumerate((hi, lo, hi)):
                            sp.dma_start(ks[r * HD1:(r + 1) * HD1, b, g, :].bitcast(F32),
                                         src[g * HD1:(g + 1) * HD1, 2, b * S:(b + 1) * S].bitcast(F32)).then_inc(k_in, 16)
                for m in range(2):
                    sp.wait_ge(lo_done, NCT * (m + 2))
                    for src, dst in ((hi, qd[0]), (lo, qd[1])):
                        sp.dma_start(dst[m * P:(m + 1) * P, :], src[:, m, :].bitcast(F32)).then_inc(q_out, 16)
                sp.wait_ge(k_in, 16 * B * G1 * 3)
                sp.wait_ge(q_out, 64)

            @block.gpsimd
            def _(pool):
                pool.memset(ks[:].bitcast(F32), 0.0).then_inc(cleared, 1)
                pool.wait_ge(cleared, 1)
                pool.memset(ks[MROW:MROW + 1, :, :, :].bitcast(F32), 1.0).then_inc(cleared, 1)
                pool.wait_ge(cleared, 2)
                pool.memset(vs[:], 0.0).then_inc(cleared, 1)
                pool.wait_ge(cleared, 3)
                pool.memset(vs[:, :, :, HD1:HD1 + 1], 1.0).then_inc(cleared, 1)
                pool.wait_ge(cleared, 4)

            @block.tensor
            def _(pe):
                pe.wait_ge(wl_done, 1)
                for n, m in enumerate((2, 0, 1)):
                    for c in range(NCT):
                        k = n * NCT + c
                        if k >= 4:
                            pe.wait_ge(lo_done, k - 3)
                            if n == 1:
                                pe.wait_ge(kv_done, c + 1)
                        for dt in range(DT):
                            i = mm3(pe, proj_ps[:, k % 4, :], wh[:, dt, m * P:(m + 1) * P], wl[:, dt, m * P:(m + 1) * P],
                                    xh[:, dt, c * CH:(c + 1) * CH], xl[:, dt, c * CH:(c + 1) * CH], dt == 0, dt == DT - 1)
                        i.then_inc(proj_done, 1)
                for c in range(NCT):
                    pe.wait_ge(kv_done, c + 1)
                    if c >= 2:
                        pe.wait_ge(v_kept, c - 1)
                    for q in range(NQ):
                        t0 = c * CH + q * P
                        i = pe.transpose(v_ps[:, c % 2, q * P:(q + 1) * P], kv[:, t0:t0 + P], ident[:])
                    i.then_inc(v_turned, 1)

            @block.scalar
            def _(act):
                act.wait_ge(w_in, 32)
                act.activation(wh[:], wr[:], ACT.Copy).then_inc(wh_done, 1)
                for n, m in enumerate((2, 0, 1)):
                    for c in range(NCT):
                        k = n * NCT + c
                        act.wait_ge(proj_done, k + 1)
                        if n == 0:
                            act.activation(kv[:, c * CH:(c + 1) * CH], proj_ps[:, k % 4, :], ACT.Identity,
                                           bias=bias[:, m:m + 1]).then_inc(kv_done, 1)
                        act.activation(hi[:, m, c * CH:(c + 1) * CH], proj_ps[:, k % 4, :], ACT.Identity,
                                       bias=bias[:, m:m + 1]).then_inc(hi_done, 1)

            @block.vector
            def _(dve):
                dve.wait_ge(wh_done, 1)
                dve.tensor_tensor(wl[:], wr[:], wh[:].bitcast(F32), ALU.subtract).then_inc(wl_done, 1)
                for n, m in enumerate((2, 0, 1)):
                    for c in range(NCT):
                        k = n * NCT + c
                        dve.wait_ge(hi_done, k + 1)
                        dve.scalar_tensor_tensor(out=lo[:, m, c * CH:(c + 1) * CH], in0=proj_ps[:, k % 4, :],
                                                 scalar=bias[:, m:m + 1], in1=hi[:, m, c * CH:(c + 1) * CH].bitcast(F32),
                                                 op0=ALU.add, op1=ALU.subtract).then_inc(lo_done, 1)
                dve.wait_ge(cleared, 4)
                for c in range(NCT):
                    dve.wait_ge(v_turned, c + 1)
                    dve.tensor_copy(vs[:, c * NQ:(c + 1) * NQ, :, 0:HD1],
                                    v_ps[:, c % 2, :].rearrange("p (q n) -> p q n", n=P)[:, :, KV1:2 * KV1]
                                    .rearrange("p q (g e) -> p q g e", e=HD1)).then_inc(v_kept, 1)

        with Phase(nc, tag + "m", psum) as am:
            qm = am.sb("qm", [P, NCH, G1, CH], F32R)
            qt = am.sb("qt", [P, NCH, G1, CH], F32R)
            pt = am.sb("pt", [P, 2, G1, 2, CH])
            part = am.sb("part", [P, 2, NQ, G1, 2])
            negm = am.sb("negm", [P, 2, NQ * G1])
            mrow = am.sb("mrow", [NQ * G1, P], F32R)
            zt = am.sb("zt", [P, CH])
            rden = am.sb("rden", [P, NQ, G1])
            st_ps = am.ps([P, 2, 2, CH])
            mx_ps = am.ps([P, 2, CH])
            acc_ps = am.ps([P, CH])
            misc_ps = am.ps([P, CH])
            cleared = am.sem("qs_cleared")
            qm_in = [am.sem(f"qm_in{s}") for s in range(2)]
            qt_in = [am.sem(f"qt_in{s}") for s in range(2)]
            m_in = [am.sem(f"m_in{s}") for s in range(2)]
            mx_ready = am.sem("mx_ready")
            mx_taken = am.sem("mx_taken")
            negm_done = am.sem("negm_done")
            m_turned = am.sem("m_turned")
            m_kept = am.sem("m_kept")
            st_ready = am.sem("st_ready")
            exp_done = am.sem("exp_done")
            pv_done = am.sem("pv_done")
            zt_done = am.sem("zt_done")
            z_turned = am.sem("z_turned")
            rden_done = am.sem("rden_done")
            z_done = am.sem("z_done")
            block = am.block()

            def walk(eng, quad, begin=None):
                if begin:
                    begin()
                for b in range(B):
                    quad(lambda c: b if c >= 0 else b - 1, 0, b * NU, b == 0, False)
                    with eng.Fori(1, QUADS - 1) as j:
                        quad(lambda c: b, j, j * NCH + b * NU, False, False)
                    quad(lambda c: b if c < NCH else b + 1, QUADS - 1, b * NU + (QUADS - 1) * NCH, False, b == B - 1)

            def first_of_all(u, least):
                return isinstance(u, int) and u < least

            @block.gpsimd
            def _(pool):
                for t in (qm, qt):
                    pool.memset(t[:].bitcast(F32), 0.0).then_inc(cleared, 1)
                pool.wait_ge(cleared, 2)

            @block.sync
            def _(sp):
                sp.wait_ge(cleared, 2)

                def fetch(dst, sem, b, j, c):
                    for r, src in enumerate((qd[0], qd[0], qd[1])):
                        rows = src[bass.ds(j * (G1 * HD1), G1 * HD1), b * S + c * CH:b * S + (c + 1) * CH]
                        sp.dma_start(dst[r * HD1:(r + 1) * HD1, c, :, :].bitcast(F32),
                                     rows.rearrange("(g p) t -> p g t", p=HD1)).then_inc(sem[c], 16)

                def quad(at, j, u0, first, last):
                    b = at(0)
                    for c in range(NCH):
                        u = u0 + c
                        if not first_of_all(u, 2):
                            sp.wait_ge(mx_ready, (u - 1) * (NQ * G1 * 2))
                        fetch(qm, qm_in, b, j, c)
                        if not first_of_all(u, 2):
                            sp.wait_ge(st_ready, (u - 1) * (NP * G1))
                        fetch(qt, qt_in, b, j, c)

                walk(sp, quad)

            def dma_count(u, c, each):
                return (u // 2 + 1) * 16 * each if isinstance(u, int) else (u + (2 - c)) * (8 * each)

            @block.tensor
            def _(pe):
                def maxima(b, u, c, q, g, half):
                    if q == 0 and g == 0 and half == 0:
                        pe.wait_ge(qm_in[c], dma_count(u, c, 3))
                    n = u * (NQ * G1 * 2) + ((q * G1 + g) * 2 + half)
                    if not first_of_all(n, 2):
                        pe.wait_ge(mx_taken, n - 1)
                    pe.matmul(mx_ps[:, half, :], qm[:, c, g, q * P:(q + 1) * P],
                              ks[:, b, g, half * CH:(half + 1) * CH], start=True, stop=True).then_inc(mx_ready, 1)

                def turn_maxima(u, c, behind=2):
                    pe.wait_ge(negm_done, u + 1)
                    if not first_of_all(u, behind + 1):
                        pe.wait_ge(z_done, u - behind)
                    pe.transpose(misc_ps[0:NQ * G1, 0:P], negm[:, c, :], ident[:]).then_inc(m_turned, 1)

                def scores(b, u, c, kp, g, k):
                    if kp == 0 and g == 0 and k == 0:
                        pe.wait_ge(qt_in[c], dma_count(u, c, 3))
                        pe.wait_ge(m_in[c], dma_count(u, c, G1))
                    n = u * (NP * G1) + (kp * G1 + g)
                    if k == 0 and not first_of_all(n, 2):
                        pe.wait_ge(exp_done, n - 1)
                    kt = kp * 2 + k
                    i = pe.matmul(st_ps[:, g % 2, k, :], ks[:, b, g, kt * P:(kt + 1) * P], qt[:, c, g, :],
                                  start=True, stop=True)
                    if k == 1:
                        i.then_inc(st_ready, 1)

                def values(b, u, kp, k):
                    if k == 0:
                        pe.wait_ge(exp_done, u * (NP * G1) + (kp + 1) * G1)
                        if kp == 0 and not first_of_all(u, 1):
                            pe.wait_ge(zt_done, u)
                    kt = kp * 2 + k
                    for g in range(G1):
                        i = pe.matmul(acc_ps[g * W:(g + 1) * W, :], vs[:, b * NK + kt, g, :], pt[:, kp % 2, g, k, :],
                                      start=kt == 0, stop=kt == NK - 1, tile_position=(0, g * W))
                    if k == 1:
                        i.then_inc(pv_done, 1)

                def turn_z(u, ahead):
                    pe.wait_ge(zt_done, u + 1)
                    pe.wait_ge(m_kept, u + ahead)
                    if ahead == 2:
                        pe.wait_ge(z_done, u)
                    for q in range(NQ):
                        i = pe.transpose(misc_ps[:, q * P:(q + 1) * P], zt[:, q * P:(q + 1) * P], ident[:])
                    i.then_inc(z_turned, 1)

                def begin():
                    for n in range(NQ * G1 * 2):
                        maxima(0, 0, 0, n // (G1 * 2), n // 2 % G1, n % 2)
                    turn_maxima(0, 0, 0)
                    for n in range(NQ // 2 * G1 * 2):
                        maxima(0, 1, 1, n // (G1 * 2), n // 2 % G1, n % 2)

                def quad(at, j, u0, first, last):
                    for c in range(NCH):
                        u = u0 + c
                        for kp in range(NP):
                            for g in range(G1):
                                for step in ORDER[g % 2]:
                                    if step == "s":
                                        scores(at(c), u, c, kp, g, 0)
                                        scores(at(c), u, c, kp, g, 1)
                                    elif step == "v":
                                        if kp > 0:
                                            values(at(c), u, kp - 1, g // 2)
                                        elif not (first and c == 0):
                                            values(at(c - 1), u - 1, NP - 1, g // 2)
                                    elif kp < 2 and not (last and c == 1):
                                        maxima(at(c + 1), u + 1, 1 - c, kp + 2, g, int(step))
                                    elif kp >= 2 and not last:
                                        maxima(at(c + 2), u + 2, c, kp - 2, g, int(step))
                            if kp == 2 and not (last and c == 1):
                                turn_maxima(u + 1, 1 - c)
                            if kp == 3 and not (first and c == 0):
                                turn_z(u - 1, 2 if last and c == 1 else 3)
                    if last:
                        for k in range(2):
                            values(at(1), u, NP - 1, k)
                        pe.wait_ge(zt_done, u + 1)
                        pe.wait_ge(z_done, u)
                        for q in range(NQ):
                            i = pe.transpose(misc_ps[:, q * P:(q + 1) * P], zt[:, q * P:(q + 1) * P], ident[:])
                        i.then_inc(z_turned, 1)

                walk(pe, quad, begin)

            @block.scalar
            def _(act):
                act.wait_ge(cleared, 2)

                def keep_maxima(u, c):
                    act.wait_ge(m_turned, u + 1)
                    if not first_of_all(u, 1):
                        act.wait_ge(m_in[1 - c], dma_count(u - 1, 1 - c, G1))
                    act.activation(mrow[:], misc_ps[0:NQ * G1, 0:P], ACT.Copy).then_inc(m_kept, 1)

                def send_maxima(u, c):
                    act.wait_ge(m_kept, u + 1)
                    if not first_of_all(u, 2):
                        act.wait_ge(st_ready, (u - 1) * (NP * G1))
                    for g in range(G1):
                        act.dma_start(qt[MROW:MROW + 1, c, g, :].bitcast(F32),
                                      mrow[g * NQ:(g + 1) * NQ, :].bitcast(F32)).then_inc(m_in[c], 16)

                def keep_z(u):
                    act.wait_ge(pv_done, (u + 1) * NP)
                    if not first_of_all(u, 1):
                        act.wait_ge(z_turned, u)
                    act.activation(zt[:], acc_ps[:], ACT.Copy).then_inc(zt_done, 1)

                def quad(at, j, u0, first, last):
                    for c in range(NCH):
                        u = u0 + c
                        for kp in range(NP):
                            for g in range(G1):
                                n = u * (NP * G1) + (kp * G1 + g)
                                act.wait_ge(st_ready, n + 1)
                                s = u * NP + kp
                                if g == 0 and not first_of_all(s, 2):
                                    act.wait_ge(pv_done, s - 1)
                                act.activation(pt[:, kp % 2, g, :, :], st_ps[:, g % 2, :, :], ACT.Exp,
                                               scale=1.0 / HD1).then_inc(exp_done, 1)
                                if kp == 3 and g == 0 and not (last and c == 1):
                                    send_maxima(u + 1, 1 - c)
                            if kp == 0 and not (first and c == 0):
                                keep_z(u - 1)
                            if kp == 2 and not (last and c == 1):
                                keep_maxima(u + 1, 1 - c)
                    if last:
                        keep_z(u)

                def begin():
                    keep_maxima(0, 0)
                    send_maxima(0, 0)

                walk(act, quad, begin)

            @block.vector
            def _(dve):
                def maxima(u, c, q):
                    for g in range(G1):
                        for half in range(2):
                            n = u * (NQ * G1 * 2) + ((q * G1 + g) * 2 + half)
                            dve.wait_ge(mx_ready, n + 1)
                            if q == 0 and g == 0 and half == 0 and not first_of_all(u, 2):
                                dve.wait_ge(negm_done, u - 1)
                            dve.tensor_reduce(part[:, c, q, g, half:half + 1], mx_ps[:, half, :], AX.X,
                                              ALU.max).then_inc(mx_taken, 1)
                    if q == NQ - 1:
                        dve.wait_ge(mx_taken, (u + 1) * (NQ * G1 * 2))
                        if not first_of_all(u, 2):
                            dve.wait_ge(m_turned, u - 1)
                        dve.tensor_reduce(negm[:, c, :].rearrange("p (g q) -> p q g", q=NQ), part[:, c, :, :, :], AX.X,
                                          ALU.max, negate=True).then_inc(negm_done, 1)

                def keep_z(b, j, u, c):
                    dve.wait_ge(z_turned, u + 1)
                    if not first_of_all(u, 1):
                        dve.wait_ge(z_done, u)
                    src = misc_ps[:].rearrange("p (q g e) -> p q g e", g=G1, e=W)
                    dve.reciprocal(rden[:], src[:, :, :, HD1]).then_inc(rden_done, 1)
                    dve.wait_ge(rden_done, u + 1)
                    t0 = b * NK + c * NQ
                    dst = z[:, t0:t0 + NQ, bass.ds(j * (G1 * HD1), G1 * HD1)].rearrange("p q (g e) -> p q g e", e=HD1)
                    dve.tensor_tensor(dst, src[:, :, :, 0:HD1],
                                      rden[:].unsqueeze(3).to_broadcast([P, NQ, G1, HD1]), ALU.mult).then_inc(z_done, 1)

                def begin():
                    for q in range(NQ):
                        maxima(0, 0, q)
                    for q in range(NQ // 2):
                        maxima(1, 1, q)

                def quad(at, j, u0, first, last):
                    for c in range(NCH):
                        u = u0 + c
                        for kp in range(NP):
                            if kp < 2 and not (last and c == 1):
                                maxima(u + 1, 1 - c, kp + 2)
                            if kp >= 2 and not last:
                                maxima(u + 2, c, kp - 2)
                            if kp == 3 and not (first and c == 0):
                                keep_z(at(c - 1), j if c else QUADS - 1 if at(-1) < at(0) else j - 1, u - 1, 1 - c)
                    if last:
                        keep_z(at(1), j, u, 1)

                walk(dve, quad, begin)

        with Phase(nc, tag + "o", psum) as op:
            wr = op.sb("wr", [P, DT, D])
            wh = op.sb("wh", [P, DT, D], F32R)
            wl = op.sb("wl", [P, DT, D], F32R)
            bias = op.sb("bias", [P, DT])
            zh = op.sb("zh", [P, DT, T], F32R)
            zl = op.sb("zl", [P, DT, T], F32R)
            idr = op.sb("idr", [P, P], F32R)
            turn_ps = op.ps([P, 4, CH])
            out_ps = op.ps([P, 4, CH])
            w_in = op.sem("w_in")
            wh_done = op.sem("wh_done")
            wl_done = op.sem("wl_done")
            turned = op.sem("turned")
            hi_done = op.sem("hi_done")
            lo_done = op.sem("lo_done")
            out_done = op.sem("out_done")
            y_done = op.sem("y_done")
            NCT = T // CH
            block = op.block()

            @block.sync
            def _(sp):
                sp.dma_start(wr[:], a["wo1"]).then_inc(w_in, 16)
                sp.dma_start(bias[:], a["bo1"]).then_inc(w_in, 16)

            @block.tensor
            def _(pe):
                def turn(c):
                    for dt in range(DT):
                        k = c * DT + dt
                        if k >= 4:
                            pe.wait_ge(lo_done, k - 3)
                        for q in range(NQ):
                            i = pe.transpose(turn_ps[:, k % 4, q * P:(q + 1) * P], z[:, c * NQ + q, dt * P:(dt + 1) * P], ident[:])
                        i.then_inc(turned, 1)

                turn(0)
                pe.wait_ge(wl_done, 1)
                for c in range(NCT):
                    if c + 1 < NCT:
                        turn(c + 1)
                    pe.wait_ge(lo_done, DT * (c + 1))
                    for m in range(DT):
                        k = c * DT + m
                        if k >= 4:
                            pe.wait_ge(y_done, k - 3)
                        o = out_ps[:, k % 4, :]
                        t = slice(c * CH, (c + 1) * CH)
                        pe.matmul(o, idr[:], xh[:, m, t], start=True, stop=False)
                        pe.matmul(o, idr[:], xl[:, m, t], start=False, stop=False)
                        for dt in range(DT):
                            i = mm3(pe, o, wh[:, dt, m * P:(m + 1) * P], wl[:, dt, m * P:(m + 1) * P],
                                    zh[:, dt, t], zl[:, dt, t], False, dt == DT - 1)
                        i.then_inc(out_done, 1)

            @block.scalar
            def _(act):
                act.wait_ge(w_in, 32)
                act.activation(wh[:], wr[:], ACT.Copy).then_inc(wh_done, 1)
                act.activation(idr[:], ident[:], ACT.Copy).then_inc(wh_done, 1)

                def keep(c):
                    for m in range(DT):
                        k = c * DT + m
                        act.wait_ge(out_done, k + 1)
                        act.activation(yT[:, m, c * CH:(c + 1) * CH], out_ps[:, k % 4, :], ACT.Identity,
                                       bias=bias[:, m:m + 1]).then_inc(y_done, 1)

                for c in range(NCT):
                    for dt in range(DT):
                        k = c * DT + dt
                        act.wait_ge(turned, k + 1)
                        act.activation(zh[:, dt, c * CH:(c + 1) * CH], turn_ps[:, k % 4, :], ACT.Copy).then_inc(hi_done, 1)
                    if c:
                        keep(c - 1)
                keep(NCT - 1)

            @block.vector
            def _(dve):
                dve.wait_ge(wh_done, 2)
                dve.tensor_tensor(wl[:], wr[:], wh[:].bitcast(F32), ALU.subtract).then_inc(wl_done, 1)
                for c in range(NCT):
                    for dt in range(DT):
                        k = c * DT + dt
                        dve.wait_ge(hi_done, k + 1)
                        dve.tensor_tensor(zl[:, dt, c * CH:(c + 1) * CH], turn_ps[:, k % 4, :],
                                          zh[:, dt, c * CH:(c + 1) * CH].bitcast(F32), ALU.subtract).then_inc(lo_done, 1)


def causal_attention(nc, tag, a, xh, xl, yT, ident, psum):
    NQ = S // P
    HB = 2 * H0
    CQ = CH // P
    SCALE = float(E0) ** -0.5
    NP = 4
    MASKED = -1.0e30
    PLAN = [[("pv", 1, True), ("q", 0)], [("k", 0)], [("o", 1, True, 0), ("o", 1, True, 1)], [("q", 1)], [("k", 1)],
            [("pv", 0, False), ("v", 0)], [("v", 1)], [("o", 0, False, 0), ("o", 0, False, 1)]]
    PROJECT = ("q", "k", "v")

    def plan(first, last):
        def wanted(t):
            return not (first and t[0] in ("pv", "o") and t[2]) and not (last and t[0] in PROJECT)
        return [[t for t in unit if wanted(t)] for unit in PLAN]

    NTASK = sum(len(u) for u in PLAN)
    NHI = sum(t[0] != "o" for u in PLAN for t in u)
    PRE = [("q", 0), ("k", 0), ("q", 1), ("k", 1), ("v", 0), ("v", 1)]
    TASKS1 = len(PRE) + sum(len(u) for u in plan(True, False))
    HIS1 = len(PRE) + sum(t[0] != "o" for u in plan(True, False) for t in u)

    def bases(hb):
        if isinstance(hb, int) and hb == 0:
            return len(PRE), len(PRE)
        return (hb - 1) * NTASK + TASKS1, (hb - 1) * NHI + HIS1

    def done_by(hb, task):
        if isinstance(hb, int) and hb == -1:
            return PRE.index(task) + 1
        first = isinstance(hb, int) and hb == 0
        last = isinstance(hb, int) and hb == HB - 1
        flat = [t for u in plan(first, last) for t in u]
        return bases(hb)[0] + flat.index(task) + 1

    def bank_of(b, first, n):
        return ((len(PRE) if first else TASKS1) + n) % 2

    NB = CQ + 2 * (NQ - CQ)

    def batches(qt):
        if qt < CQ:
            return [(0, qt + 1, qt)]
        n = CQ + 2 * (qt - CQ)
        return [(0, CQ, n), (CQ, qt + 1 - CQ, n + 1)]

    with Phase(nc, tag, psum) as ph:
        wr = ph.sb("wr", [P, 2, 3, DT, E0])
        wh = ph.sb("wh", [P, 2, 3, DT, E0], F32R)
        wl = ph.sb("wl", [P, 2, 3, DT, E0], F32R)
        wor = ph.sb("wor", [P, D])
        woh = ph.sb("woh", [P, D], F32R)
        wol = ph.sb("wol", [P, D], F32R)
        qh = ph.sb("qh", [P, B, S], F32R)
        ql = ph.sb("ql", [P, B, S], F32R)
        kh = ph.sb("kh", [P, B, S], F32R)
        kl = ph.sb("kl", [P, B, S], F32R)
        vh = ph.sb("vh", [P, B, NQ, E0], F32R)
        vl = ph.sb("vl", [P, B, NQ, E0], F32R)
        pr = ph.sb("pr", [P, NP, S])
        pth = [ph.sb(f"pth{c}", [P, CQ * (c + 1), CH], F32R) for c in range(2)]
        ptl = [ph.sb(f"ptl{c}", [P, CQ * (c + 1), CH], F32R) for c in range(2)]
        zh = ph.sb("zh", [P, 2, CH], F32R)
        zl = ph.sb("zl", [P, 2, CH], F32R)
        negm = ph.sb("negm", [P, NP])
        rsum = ph.sb("rsum", [P, NP])
        rinv = ph.sb("rinv", [P, NP])
        mask0 = ph.sb("mask0", [P, P])
        mask = ph.sb("mask", [P, P], F32R)
        idr = ph.sb("idr", [P, P], F32R)
        s_ps = ph.ps([P, 2, S])
        t_ps = ph.ps([P, 2, CH])
        r_ps = ph.ps([P, 2, CH])
        cleared = ph.sem("cleared")
        mask_set = ph.sem("mask_set")
        rounded = ph.sem("rounded")
        wr_in = [ph.sem(f"wr_in{s}") for s in range(2)]
        wh_done = ph.sem("wh_done")
        wl_done = ph.sem("wl_done")
        wor_in = ph.sem("wor_in")
        woh_done = ph.sem("woh_done")
        wol_done = ph.sem("wol_done")
        s_ready = ph.sem("s_ready")
        max_done = ph.sem("max_done")
        exp_done = ph.sem("exp_done")
        inv_done = ph.sem("inv_done")
        p_done = ph.sem("p_done")
        t_ready = ph.sem("t_ready")
        th_done = ph.sem("th_done")
        tl_done = ph.sem("tl_done")
        task_done = ph.sem("task_done")
        task_hi = ph.sem("task_hi")
        task_out = ph.sem("task_out")
        block = ph.block()

        def walk(eng, half, begin=None, end=None):
            if begin:
                begin()
            half(0, 0, 0, True, False)
            with eng.Fori(0, H0 - 2) as h:
                half(h * 2 + 1, h, 1, False, False)
                half(h * 2 + 2, h + 1, 0, False, False)
            half(HB - 3, H0 - 2, 1, False, False)
            half(HB - 2, H0 - 1, 0, False, False)
            half(HB - 1, H0 - 1, 1, False, True)
            if end:
                end()

        def at_least(n, least):
            return not isinstance(n, int) or n >= least

        def pair_of(task, b):
            kind, c = task[0], task[1]
            t = slice(c * CH, (c + 1) * CH)
            if kind == "q":
                return qh[:, 1 - b, t], ql[:, 1 - b, t]
            if kind == "k":
                return kh[:, 1 - b, t], kl[:, 1 - b, t]
            if kind == "v":
                t = slice(c * CQ, (c + 1) * CQ)
                return (vh[:, 1 - b, t, :].rearrange("p t e -> p (t e)"), vl[:, 1 - b, t, :].rearrange("p t e -> p (t e)"))
            return zh[:, c, :], zl[:, c, :]

        @block.sync
        def _(sp):
            def load(n, s, h):
                if at_least(n, 2):
                    sp.wait_ge(wl_done, n - 1)
                sp.dma_start(wr[:, s], a["qkv0"][bass.ds(h, 1)].rearrange("o p w t e -> (o p) w t e")).then_inc(wr_in[s], 16)

            def load_o(h):
                if at_least(h, 1):
                    sp.wait_ge(wol_done, h)
                sp.dma_start(wor[:], a["o0"][bass.ds(h, 1)].rearrange("o e d -> (o e) d")).then_inc(wor_in, 16)

            load(0, 0, 0)
            load(1, 1, 0)
            load_o(0)
            with sp.Fori(1, H0) as h:
                load(h * 2, 0, h)
                load(h * 2 + 1, 1, h)
                load_o(h)

        @block.gpsimd
        def _(pool):
            def split(n, s):
                pool.wait_ge(wh_done, n + 1)
                pool.tensor_tensor(wl[:, s].rearrange("p w t e -> p (w t e)"), wr[:, s].rearrange("p w t e -> p (w t e)"),
                                   wh[:, s].rearrange("p w t e -> p (w t e)").bitcast(F32),
                                   ALU.subtract).then_inc(wl_done, 1)

            def split_o(h):
                pool.wait_ge(woh_done, h + 1)
                pool.tensor_tensor(wol[:], wor[:], woh[:].bitcast(F32), ALU.subtract).then_inc(wol_done, 1)

            pool.memset(mask0[:], 0.0).then_inc(cleared, 1)
            pool.wait_ge(cleared, 1)
            pool.affine_select(out=mask0[:], in_=mask0[:], compare_op=ALU.is_ge, fill=MASKED, base=0,
                               pattern=[[-1, P]], channel_multiplier=1).then_inc(mask_set, 1)
            split(0, 0)
            split(1, 1)
            split_o(0)
            split(2, 0)
            with pool.Fori(1, H0 - 1) as h:
                split(h * 2 + 1, 1)
                split(h * 2 + 2, 0)
                split_o(h)
            split(HB - 1, 1)
            split_o(H0 - 1)

        @block.tensor
        def _(pe):
            def scores(hb, b, qt):
                u = hb * NQ + qt
                if qt == 0:
                    pe.wait_ge(task_out, done_by(hb - 1, ("k", 0)))
                if qt == CQ:
                    pe.wait_ge(task_out, done_by(hb - 1, ("k", 1)))
                if at_least(u, 2):
                    pe.wait_ge(exp_done, u - 1)
                q0 = qt * P
                keys = q0 + P
                for k0 in range(0, keys, CH):
                    k1 = min(keys, k0 + CH)
                    o = s_ps[:, qt % 2, k0:k1]
                    i = mm3(pe, o, qh[:, b, q0:q0 + P], ql[:, b, q0:q0 + P], kh[:, b, k0:k1], kl[:, b, k0:k1],
                            True, k1 < keys)
                i = pe.matmul(s_ps[:, qt % 2, q0:q0 + P], idr[:], mask[:], start=False, stop=True)
                i.then_inc(s_ready, 1)

            def turn(hb, qt):
                pe.wait_ge(p_done, hb * NQ + (qt + 1))
                for k0, count, n in batches(qt):
                    m = hb * NB + n
                    if at_least(m, 2):
                        pe.wait_ge(tl_done, m - 1)
                    for k in range(count):
                        i = pe.transpose(t_ps[:, n % 2, k * P:(k + 1) * P], pr[:, qt % NP, (k0 + k) * P:(k0 + k + 1) * P],
                                         ident[:])
                    i.then_inc(t_ready, 1)

            def task(hb, h, b, t, k, bank):
                if at_least(k, 2):
                    pe.wait_ge(task_out, k - 1)
                o = r_ps[:, bank, :]
                kind, c = t[0], t[1]
                nb = 1 - b
                x0 = nb * S + c * CH
                if kind in ("q", "k"):
                    if kind == "q" and c == 0:
                        pe.wait_ge(wl_done, hb + 2)
                    w = PROJECT.index(kind)
                    for dt in range(DT):
                        i = mm3(pe, o, wh[:, nb, w, dt, :], wl[:, nb, w, dt, :], xh[:, dt, x0:x0 + CH], xl[:, dt, x0:x0 + CH],
                                dt == 0, dt == DT - 1)
                elif kind == "v":
                    for q in range(CQ):
                        t0 = x0 + q * P
                        for dt in range(DT):
                            i = mm3(pe, o[:, q * P:(q + 1) * P], xh[:, dt, t0:t0 + P], xl[:, dt, t0:t0 + P],
                                    wh[:, nb, 2, dt, :], wl[:, nb, 2, dt, :], dt == 0, dt == DT - 1)
                elif kind == "pv":
                    hs, vb = (hb - 1, nb) if t[2] else (hb, b)
                    pe.wait_ge(tl_done, hs * NB + (NB if c else CQ))
                    if c == 0:
                        pe.wait_ge(task_out, done_by(hs - 1, ("v", 1)))
                    for kt in range(CQ * (c + 1)):
                        q0 = max(0, kt - CQ * c) * P
                        i = mm3(pe, o[:, q0:CH], vh[:, vb, kt, :], vl[:, vb, kt, :], pth[c][:, kt, q0:CH], ptl[c][:, kt, q0:CH],
                                kt == 0, kt == CQ * (c + 1) - 1)
                else:
                    dt = t[3]
                    if dt == 0:
                        pe.wait_ge(task_out, done_by(hb, ("pv", c, t[2])))
                        if not (t[2]):
                            pe.wait_ge(wol_done, h + 1)
                    i = mm3(pe, o, woh[:, dt * P:(dt + 1) * P], wol[:, dt * P:(dt + 1) * P], zh[:, c, :], zl[:, c, :],
                            True, True)
                i.then_inc(task_done, 1)

            def half(hb, h, b, first, last):
                k, n = bases(hb)[0], 0
                for qt, tasks in enumerate(plan(first, last)):
                    if qt < NQ - 2:
                        scores(hb, b, qt + 2)
                    elif not last:
                        scores(hb + 1, 1 - b, qt + 2 - NQ)
                    turn(hb, qt)
                    for t in tasks:
                        task(hb, h, b, t, k + n, bank_of(b, first, n))
                        n += 1

            def begin():
                pe.wait_ge(rounded, 2)
                for n, t in enumerate(PRE):
                    task(-1, 0, 1, t, n, n % 2)
                for qt in range(2):
                    scores(0, 0, qt)

            def end():
                k, n0 = last_tasks
                for n, t in enumerate([("pv", 1, True), ("o", 1, True, 0), ("o", 1, True, 1)]):
                    if t[0] == "o" and t[3] == 0:
                        pe.wait_ge(task_out, k + 1)
                    finish(t, k + n)

            last_tasks = (bases(HB - 1)[0] + sum(len(u) for u in plan(False, True)), None)

            def finish(t, k):
                pe.wait_ge(task_out, k - 1)
                o = r_ps[:, k % 2, :]
                if t[0] == "pv":
                    pe.wait_ge(tl_done, HB * NB)
                    for kt in range(NQ):
                        q0 = max(0, kt - CQ) * P
                        i = mm3(pe, o[:, q0:CH], vh[:, 1, kt, :], vl[:, 1, kt, :], pth[1][:, kt, q0:CH], ptl[1][:, kt, q0:CH],
                                kt == 0, kt == NQ - 1)
                else:
                    dt = t[3]
                    i = mm3(pe, o, woh[:, dt * P:(dt + 1) * P], wol[:, dt * P:(dt + 1) * P], zh[:, 1, :], zl[:, 1, :],
                            True, True)
                i.then_inc(task_done, 1)

            walk(pe, half, begin, end)

        @block.scalar
        def _(act):
            def soften(hb, qt):
                u = hb * NQ + qt
                act.wait_ge(max_done, u + 1)
                if at_least(u, NP):
                    nb = qt - NP if qt >= NP else qt - NP + NQ
                    hp = hb if qt >= NP else hb - 1
                    act.wait_ge(t_ready, hp * NB + (batches(nb)[-1][2] + 1))
                n = (qt + 1) * P
                act.activation(pr[:, qt % NP, 0:n], s_ps[:, qt % 2, 0:n], ACT.Exp, bias=negm[:, qt % NP:qt % NP + 1],
                               accum_out=rsum[:, qt % NP:qt % NP + 1]).then_inc(exp_done, 1)

            def keep_hi(hb, qt):
                for k0, count, n in batches(qt):
                    act.wait_ge(t_ready, hb * NB + (n + 1))
                    c, q0 = qt // CQ, (qt % CQ) * P
                    act.activation(pth[c][:, k0:k0 + count, q0:q0 + P],
                                   t_ps[:, n % 2, 0:count * P].rearrange("p (k q) -> p k q", q=P), ACT.Copy).then_inc(th_done, 1)

            def round_weights(s, count):
                act.wait_ge(wr_in[s], count)
                act.activation(wh[:, s], wr[:, s], ACT.Copy).then_inc(wh_done, 1)

            def round_o(h):
                act.wait_ge(wor_in, (h + 1) * 16)
                if at_least(h, 1):
                    act.wait_ge(task_done, done_by(h * 2, ("o", 1, True, 1)))
                act.activation(woh[:], wor[:], ACT.Copy).then_inc(woh_done, 1)

            def task(b, t, k, bank):
                act.wait_ge(task_done, k + 1)
                act.activation(pair_of(t, b)[0], r_ps[:, bank, :], ACT.Copy,
                               scale=SCALE if t[0] == "q" else 1.0).then_inc(task_hi, 1)

            def half(hb, h, b, first, last):
                k, n = bases(hb)[0], 0
                for qt, tasks in enumerate(plan(first, last)):
                    keep_hi(hb, qt)
                    if qt < NQ - 2:
                        soften(hb, qt + 2)
                    elif not last:
                        soften(hb + 1, qt + 2 - NQ)
                    for t in tasks:
                        if t[0] != "o":
                            task(b, t, k + n, bank_of(b, first, n))
                        n += 1
                    if qt == 3:
                        if not isinstance(hb, int) or hb < HB - 2:
                            round_weights(b, (h + 2) * 16)
                        if b == 0 and not first:
                            round_o(h)

            def begin():
                round_weights(0, 16)
                round_weights(1, 16)
                round_o(0)
                act.wait_ge(mask_set, 1)
                act.activation(mask[:], mask0[:], ACT.Copy).then_inc(rounded, 1)
                act.activation(idr[:], ident[:], ACT.Copy).then_inc(rounded, 1)
                for n, t in enumerate(PRE):
                    task(1, t, n, n % 2)
                for qt in range(2):
                    soften(0, qt)

            def end():
                k = bases(HB - 1)[0] + sum(len(u) for u in plan(False, True))
                task(0, ("pv", 1, True), k, k % 2)

            walk(act, half, begin, end)

        @block.vector
        def _(dve):
            def maximum(hb, qt):
                u = hb * NQ + qt
                dve.wait_ge(s_ready, u + 1)
                n = (qt + 1) * P
                dve.tensor_reduce(negm[:, qt % NP:qt % NP + 1], s_ps[:, qt % 2, 0:n], AX.X, ALU.max,
                                  negate=True).then_inc(max_done, 1)

            def normalise(hb, qt):
                u = hb * NQ + qt
                j = qt % NP
                dve.wait_ge(exp_done, u + 1)
                dve.reciprocal(rinv[:, j:j + 1], rsum[:, j:j + 1]).then_inc(inv_done, 1)
                dve.wait_ge(inv_done, u + 1)
                n = (qt + 1) * P
                dve.tensor_scalar(pr[:, j, 0:n], pr[:, j, 0:n], rinv[:, j:j + 1], None, ALU.mult).then_inc(p_done, 1)

            def keep_lo(hb, qt):
                for k0, count, n in batches(qt):
                    dve.wait_ge(th_done, hb * NB + (n + 1))
                    c, q0 = qt // CQ, (qt % CQ) * P
                    dve.tensor_tensor(ptl[c][:, k0:k0 + count, q0:q0 + P],
                                      t_ps[:, n % 2, 0:count * P].rearrange("p (k q) -> p k q", q=P),
                                      pth[c][:, k0:k0 + count, q0:q0 + P].bitcast(F32), ALU.subtract).then_inc(tl_done, 1)

            def task(b, t, k, hi, bank):
                src = r_ps[:, bank, :]
                if t[0] == "o":
                    dve.wait_ge(task_done, k + 1)
                    ob = 1 - b if t[2] else b
                    y = yT[:, t[3], ob * S + t[1] * CH:ob * S + (t[1] + 1) * CH]
                    if at_least(k, NTASK):
                        dve.wait_ge(task_out, k - NTASK + 1)
                    dve.tensor_tensor(y, y, src, ALU.add).then_inc(task_out, 1)
                    return
                dve.wait_ge(task_hi, hi + 1)
                h, l = pair_of(t, b)
                if t[0] == "q":
                    dve.scalar_tensor_tensor(out=l, in0=src, scalar=SCALE, in1=h.bitcast(F32), op0=ALU.mult,
                                             op1=ALU.subtract).then_inc(task_out, 1)
                else:
                    dve.tensor_tensor(l, src, h.bitcast(F32), ALU.subtract).then_inc(task_out, 1)

            def half(hb, h, b, first, last):
                (k, hi), n, m = bases(hb), 0, 0
                for qt, tasks in enumerate(plan(first, last)):
                    if qt < NQ - 1:
                        normalise(hb, qt + 1)
                    elif not last:
                        normalise(hb + 1, 0)
                    if qt < NQ - 2:
                        maximum(hb, qt + 2)
                    elif not last:
                        maximum(hb + 1, qt + 2 - NQ)
                    keep_lo(hb, qt)
                    for t in tasks:
                        task(b, t, k + n, hi + m, bank_of(b, first, n))
                        m += t[0] != "o"
                        n += 1

            def begin():
                for n, t in enumerate(PRE):
                    task(1, t, n, n, n % 2)
                for qt in range(2):
                    maximum(0, qt)
                normalise(0, 0)

            def end():
                k = bases(HB - 1)[0] + sum(len(u) for u in plan(False, True))
                hi = bases(HB - 1)[1] + sum(t[0] != "o" for u in plan(False, True) for t in u)
                for n, t in enumerate([("pv", 1, True), ("o", 1, True, 0), ("o", 1, True, 1)]):
                    task(0, t, k + n, hi, (k + n) % 2)

            walk(dve, half, begin, end)


def prepare(nc, tag, xT, xh, xl, yT, ident):
    with Phase(nc, tag) as ph:
        y_in = [ph.sem(f"y_in{c}") for c in range(T // CH)]
        cleared = ph.sem("cleared")
        ident_done = ph.sem("ident_done")
        hi_done = ph.sem("hi_done")
        lo_done = ph.sem("lo_done")
        block = ph.block()

        @block.sync
        def _(sp):
            for c in range(T // CH):
                t = slice(c * CH, (c + 1) * CH)
                sp.dma_start(yT[:, :, t], xT[:, :, t]).then_inc(y_in[c], 16)

        @block.gpsimd
        def _(pool):
            pool.memset(ident[:], 0.0).then_inc(cleared, 1)
            pool.wait_ge(cleared, 1)
            pool.affine_select(out=ident[:], in_=ident[:], compare_op=ALU.not_equal, fill=1.0, base=0,
                               pattern=[[-1, P]], channel_multiplier=1).then_inc(ident_done, 1)
            pool.wait_ge(ident_done, 1)

        @block.scalar
        def _(act):
            for c in range(T // CH):
                t = slice(c * CH, (c + 1) * CH)
                act.wait_ge(y_in[c], 16)
                act.activation(xh[:, :, t], yT[:, :, t], ACT.Copy).then_inc(hi_done, 1)

        @block.vector
        def _(dve):
            for c in range(T // CH):
                t = slice(c * CH, (c + 1) * CH)
                dve.wait_ge(hi_done, c + 1)
                dve.tensor_tensor(xl[:, :, t], yT[:, :, t], xh[:, :, t].bitcast(F32), ALU.subtract).then_inc(lo_done, 1)
            dve.wait_ge(lo_done, T // CH)


def program(nc, a, out):
    with ExitStack() as stack:
        def sb(name, shape, dt=F32):
            return stack.enter_context(nc.sbuf_tensor(name, shape, dt))

        xh = sb("xh", [P, DT, T], F32R)
        xl = sb("xl", [P, DT, T], F32R)
        yT = sb("yT", [P, DT, T])
        ident = sb("ident", [P, P])
        psum = stack.enter_context(nc.psum_tensor("psum", [P, 8, CH], F32))
        rows = out.rearrange("b s d -> (b s) d")
        norm_sems = layer_norm_semaphores(nc, stack)
        prepare(nc, "in", a["xT"], xh, xl, yT, ident)

        causal_attention(nc, "a0", a, xh, xl, yT, ident, psum)
        layer_norm(nc, "n0", 0, norm_sems, yT, xh, xl, ident, psum)

        w = {"groups": 1, "shared_tiles": NSH0, "topk": 2, "gate_w": a["gw0"], "gate_b": None, "sel": a["sel0"],
             "gu": a["gu0"], "down": a["down0"]}
        mixture(nc, "f0", w, xh, xl, yT, ident, psum, True)
        layer_norm(nc, "n1", 1, norm_sems, yT, xh, xl, ident, psum)

        grouped_attention(nc, "a1", a, xh, xl, yT, ident, psum)
        layer_norm(nc, "n2", 2, norm_sems, yT, xh, xl, ident, psum)

        w = {"groups": 2, "shared_tiles": NSH1, "topk": 6, "gate_w": a["gw1"], "gate_b": a["gb1"], "sel": a["sel1"],
             "gu": a["gu1"], "down": a["down1"], "b2": a["b21"]}
        mixture(nc, "f1", w, xh, xl, yT, ident, psum, False)
        layer_norm(nc, "n3", 3, norm_sems, yT, xh, xl, ident, psum, rows)


def by_tiles(w, groups, shared, nsh):
    n = w.shape[2]
    e = w.reshape(groups, NE, NJ, SLICE, n).transpose(0, 2, 1, 3, 4).reshape(groups * NJ, P, n)
    s = np.zeros((nsh * P, n), w.dtype)
    s[:shared.shape[0]] = shared
    return np.concatenate([e, s.reshape(nsh, P, n)])


def by_inputs(t):
    return t.reshape(t.shape[0], P, DT, P).transpose(0, 3, 2, 1)


def pack_ffn(gate, up, down, sgate, sup, sdown, groups, nsh, b_gate=None, b_up=None, sb_gate=None, sb_up=None):
    nt = groups * NJ + nsh
    g = by_inputs(by_tiles(gate, groups, sgate, nsh)).reshape(nt, P, DT * P)
    u = by_inputs(by_tiles(up, groups, sup, nsh)).reshape(nt, P, DT * P)
    if b_gate is None:
        bias = np.zeros((nt, P, 2), gate.dtype)
    else:
        bias = np.concatenate([by_tiles(b_gate[:, :, None], groups, sb_gate[:, None], nsh),
                               by_tiles(b_up[:, :, None], groups, sb_up[:, None], nsh)], axis=2)
    return np.concatenate([g, u, bias], axis=2), by_tiles(down, groups, sdown, nsh)


def selectors(groups, gate):
    ne = NE * groups
    sel = np.zeros((ne + 1, groups + (1 if gate else 0), P), np.float32)
    for e in range(ne):
        sel[e, e // NE, (e % NE) * SLICE:(e % NE + 1) * SLICE] = 1
    if gate:
        sel[ne, groups, :] = 1
    return sel


def inner(m):
    return m.reshape(DT, P, m.shape[1]).transpose(1, 0, 2)


def layouts(i):
    i = {k: np.asarray(v) for k, v in i.items()}
    a = {"xT": inner(i["L0_attn_x"].reshape(T, D).T)}
    a["qkv0"] = np.stack([w.transpose(0, 2, 1).reshape(H0, DT, P, E0).transpose(0, 2, 1, 3)
                          for w in (i["L0_attn_W_Q"], i["L0_attn_W_K"], i["L0_attn_W_V"])], axis=2)
    a["o0"] = i["L0_attn_W_O"].transpose(0, 2, 1)
    a["gu0"], a["down0"] = pack_ffn(i["L0_ffn_w_gate"].transpose(0, 2, 1), i["L0_ffn_w_up"].transpose(0, 2, 1),
                                    i["L0_ffn_w_down"], i["L0_ffn_sw_gate"].T, i["L0_ffn_sw_up"].T,
                                    i["L0_ffn_sw_down"], 1, NSH0)
    pad = np.zeros((1, D), np.float32)
    a["gw0"] = inner(np.concatenate([i["L0_ffn_gate_w"], i["L0_ffn_shared_gate_w"].T, pad]).T)
    a["sel0"] = selectors(1, True)
    a["gu1"], a["down1"] = pack_ffn(i["L1_ffn_w1"], i["L1_ffn_w3"], i["L1_ffn_w2"].transpose(0, 2, 1),
                                    i["L1_ffn_ws1"], i["L1_ffn_ws3"], i["L1_ffn_ws2"].T, 2, NSH1,
                                    i["L1_ffn_b1"], i["L1_ffn_b3"], i["L1_ffn_bs1"], i["L1_ffn_bs3"])
    a["gw1"] = inner(i["L1_ffn_gate_w"].T)
    a["gb1"] = np.broadcast_to(i["L1_ffn_gate_b"], (P, 2 * NE))
    a["b21"] = np.concatenate([i["L1_ffn_b2"], i["L1_ffn_bs2"][None]])
    a["sel1"] = selectors(2, False)
    a["wqkv1"] = inner(i["L1_attn_Wqkv"])
    a["bqkv1"] = i["L1_attn_bqkv"].reshape(3, P).T
    a["wo1"] = inner(i["L1_attn_Wout"])
    a["bo1"] = i["L1_attn_bout"].reshape(DT, P).T
    return {k: np.ascontiguousarray(v) for k, v in a.items()}


def kernel(**inputs):
    import concourse.bacc as _bacc
    from concourse.bass_utils import run_bass_kernel_spmd as _run

    nc = _bacc.Bacc("TRN2", target_bir_lowering=False, num_devices=1)
    arrays, aps = {}, {}
    for name, v in layouts(inputs).items():
        arrays[f"in_{name}"] = v
        aps[name] = nc.dram_tensor(f"in_{name}", v.shape, mybir.dt.from_np(v.dtype), kind="ExternalInput").ap()
    out = nc.dram_tensor("out", (B, S, D), F32, kind="ExternalOutput").ap()
    program(nc, aps, out)
    return _run(nc, [arrays], core_ids=[0]).results[0]["out"]
```

```python
from contextlib import ExitStack

import numpy as np

import concourse.bass as bass
from concourse import mybir

F32 = mybir.dt.float32
F32R = mybir.dt.float32r
ACT = mybir.ActivationFunctionType
ALU = mybir.AluOpType
AX = mybir.AxisListType

P = 128
B, S, D = 2, 1024, 256
T = B * S
DT = D // P
NTOK = T // P
CH = 512
EPS = 1e-5

H0, E0 = 16, 128
H1, HD1, G1 = 16, 16, 4
KV1 = HD1 * G1

NE = 8
INTER = 176
SLICE = P // NE
NJ = INTER // SLICE
HS0, HS1 = 704, 352
NSH0, NSH1 = -(-HS0 // P), -(-HS1 // P)


class Phase:

    def __init__(self, nc, tag, psum=None):
        self.nc, self.tag, self.stack, self.psum, self.bank = nc, tag, ExitStack(), psum, 0

    def __enter__(self):
        return self

    def __exit__(self, *a):
        self.stack.close()

    def sb(self, name, shape, dt=F32):
        return self.stack.enter_context(self.nc.sbuf_tensor(f"{self.tag}_{name}", shape, dt))

    def ps(self, shape):
        size = int(np.prod(shape[1:]))
        banks = size // CH
        b0, self.bank = self.bank, self.bank + banks
        assert size == banks * CH and self.bank <= 8
        flat = self.psum[0:shape[0], b0:b0 + banks, :].rearrange("p b n -> p (b n)")
        names = " ".join(f"d{k}" for k in range(len(shape) - 1))
        return flat.rearrange(f"p ({names}) -> p {names}", **{f"d{k}": n for k, n in enumerate(shape[1:])})

    def sem(self, name):
        return self.stack.enter_context(self.nc.semaphore(f"{self.tag}_{name}"))

    def block(self):
        return self.stack.enter_context(self.nc.Block())


def mm3(pe, out, a_hi, a_lo, b_hi, b_lo, first, last):
    pe.matmul(out, a_hi, b_hi, start=first, stop=False)
    pe.matmul(out, a_hi, b_lo, start=False, stop=False)
    return pe.matmul(out, a_lo, b_hi, start=False, stop=last)


def layer_norm_semaphores(nc, stack):
    names = ("eps_set", "y_turned", "stats_done", "mv_done", "std_done", "rstd_done", "xn_done", "x_turned",
             "hi_done", "lo_done", "stored0", "stored1")
    return {name: stack.enter_context(nc.semaphore(f"norm_{name}")) for name in names}


def layer_norm(nc, tag, nth, sems, yT, xh, xl, ident, psum, out=None):
    Q = 4
    NG = NTOK // Q
    with Phase(nc, tag, psum) as ph:
        tok = ph.ps([P, 2, Q, D])
        back = ph.ps([P, 2, DT, Q * P])
        stats = ph.sb("stats", [P, Q, 6])
        mv = ph.sb("mv", [P, Q, 2])
        std = ph.sb("std", [P, Q])
        rstd = ph.sb("rstd", [P, Q])
        eps = ph.sb("eps", [P, 1])
        xn = ph.sb("xn", [P, 2, Q, D])
        eps_set, y_turned, stats_done, mv_done = (sems[n] for n in ("eps_set", "y_turned", "stats_done", "mv_done"))
        std_done, rstd_done, xn_done = (sems[n] for n in ("std_done", "rstd_done", "xn_done"))
        x_turned, hi_done, lo_done = (sems[n] for n in ("x_turned", "hi_done", "lo_done"))
        stored = [sems["stored0"], sems["stored1"]]
        G0, T0, D0 = nth * NG, nth * NTOK, nth * NG * DT
        block = ph.block()

        @block.tensor
        def _(pe):
            def turn_y(g):
                if g >= 2:
                    pe.wait_ge(xn_done, T0 + Q * (g - 1))
                for q in range(Q):
                    for dt in range(DT):
                        t0 = (g * Q + q) * P
                        m = pe.transpose(tok[:, g % 2, q, dt * P:(dt + 1) * P], yT[:, dt, t0:t0 + P], ident[:])
                    m.then_inc(y_turned, 1)

            def turn_x(g):
                if g >= 2:
                    pe.wait_ge(lo_done, D0 + DT * (g - 1))
                for q in range(Q):
                    pe.wait_ge(xn_done, T0 + g * Q + q + 1)
                    for dt in range(DT):
                        m = pe.transpose(back[:, g % 2, dt, q * P:(q + 1) * P],
                                         xn[:, g % 2, q, dt * P:(dt + 1) * P], ident[:])
                m.then_inc(x_turned, 1)

            turn_y(0)
            for g in range(NG):
                if g + 1 < NG:
                    turn_y(g + 1)
                if out is None:
                    turn_x(g)

        @block.vector
        def _(dve):
            dve.memset(eps[:], EPS).then_inc(eps_set, 1)

            def take_stats(g):
                dve.wait_ge(y_turned, T0 + Q * (g + 1))
                if g >= 1:
                    dve.wait_ge(mv_done, T0 + Q * g)
                    dve.wait_ge(xn_done, T0 + Q * g)
                for q in range(Q):
                    dve.bn_stats(stats[:, q, :], tok[:, g % 2, q, :]).then_inc(stats_done, 1)
                for q in range(Q):
                    dve.wait_ge(stats_done, T0 + g * Q + q + 1)
                    dve.bn_aggr(mv[:, q, :], stats[:, q, :]).then_inc(mv_done, 1)

            def normalise(g):
                dve.wait_ge(std_done, G0 + g + 1)
                dve.reciprocal(rstd[:], std[:]).then_inc(rstd_done, 1)
                dve.wait_ge(rstd_done, G0 + g + 1)
                if g >= 2:
                    if out is None:
                        dve.wait_ge(x_turned, G0 + g - 1)
                    else:
                        dve.wait_ge(stored[g % 2], 16 * (g // 2))
                for q in range(Q):
                    dve.tensor_scalar(xn[:, g % 2, q, :], tok[:, g % 2, q, :], mv[:, q, 0:1], rstd[:, q:q + 1],
                                      ALU.subtract, ALU.mult).then_inc(xn_done, 1)

            def keep_lo(g):
                for dt in range(DT):
                    dve.wait_ge(hi_done, D0 + g * DT + dt + 1)
                    t0 = g * Q * P
                    dve.tensor_tensor(xl[:, dt, t0:t0 + Q * P], back[:, g % 2, dt, :], xh[:, dt, t0:t0 + Q * P].bitcast(F32),
                                      ALU.subtract).then_inc(lo_done, 1)

            for g in range(NG):
                take_stats(g)
                if out is None and g >= 1:
                    keep_lo(g - 1)
                normalise(g)
            if out is None:
                keep_lo(NG - 1)

        @block.scalar
        def _(act):
            def root(g):
                act.wait_ge(mv_done, T0 + Q * (g + 1))
                if g >= 1:
                    act.wait_ge(rstd_done, G0 + g)
                act.activation(std[:], mv[:, :, 1], ACT.Sqrt, bias=eps[:, 0:1]).then_inc(std_done, 1)

            act.wait_ge(eps_set, nth + 1)
            for g in range(NG):
                root(g)
                if out is None:
                    act.wait_ge(x_turned, G0 + g + 1)
                    t0 = g * Q * P
                    for dt in range(DT):
                        act.activation(xh[:, dt, t0:t0 + Q * P], back[:, g % 2, dt, :], ACT.Copy).then_inc(hi_done, 1)

        if out is not None:
            @block.sync
            def _(sp):
                rows = out.rearrange("(g q p) d -> g p q d", q=Q, p=P)
                for g in range(NG):
                    sp.wait_ge(xn_done, T0 + Q * (g + 1))
                    sp.dma_start(rows[g], xn[:, g % 2, :, :]).then_inc(stored[g % 2], 16)
                for s in range(2):
                    sp.wait_ge(stored[s], 16 * (NG // 2))


def mixture(nc, tag, w, xh, xl, yT, ident, psum, shared_gate):
    groups = w["groups"]
    ne = NE * groups
    nr = ne + (2 if shared_gate else 0)
    nsh = w["shared_tiles"]
    topk = w["topk"]
    biased = w["gate_b"] is not None
    nmap = groups + (1 if shared_gate else 0)
    NT = groups * NJ + nsh
    unmapped = 0 if shared_gate else nsh
    HALF = T // 2
    NC = HALF // CH

    with Phase(nc, tag, psum) as ph:
        cmap = ph.sb("cmap", [P, nmap, T])
        cTh = ph.sb("cTh", [ne + 1, T], F32R)
        cTl = ph.sb("cTl", [ne + 1, T], F32R)

        with Phase(nc, tag + "r", psum) as rt:
            gw = rt.sb("gw", [P, DT, nr])
            gwh = rt.sb("gwh", [P, DT, nr], F32R)
            gwl = rt.sb("gwl", [P, DT, nr], F32R)
            sel = rt.sb("sel", [ne + 1, nmap, P])
            selr = rt.sb("selr", [ne + 1, nmap, P], F32R)
            gb = rt.sb("gb", [P, ne])
            lg_bank = rt.ps([P, CH])
            lg_ps = lg_bank[:, 0:NTOK * nr].rearrange("p (t n) -> p t n", n=nr)
            wide_ps = rt.ps([P, 4, CH])
            turn_ps, map_ps = wide_ps[0:ne + 1, 0:2, :], wide_ps[:, 2:4, :]
            lgT = rt.sb("lgT", [nr, T])
            lg = rt.sb("lg", [P, NTOK, nr])
            mx = rt.sb("mx", [P, NTOK])
            sh = rt.sb("sh", [P, NTOK, ne])
            ex = rt.sb("ex", [P, NTOK, ne])
            sg = rt.sb("sg", [P, NTOK])
            sm = rt.sb("sm", [P, NTOK])
            pr = rt.sb("pr", [P, NTOK, ne])
            bi = rt.sb("bi", [P, NTOK, ne])
            top = rt.sb("top", [P, NTOK, 8])
            rest = rt.sb("rest", [P, NTOK, ne])
            cw = rt.sb("cw", [P, NTOK, ne + 1])
            loaded = rt.sem("loaded")
            hi_done = rt.sem("hi_done")
            lo_done = rt.sem("lo_done")
            lgT_done = rt.sem("lgT_done")
            lgT_kept = rt.sem("lgT_kept")
            logits_done = rt.sem("logits_done")
            shifted = rt.sem("shifted")
            exp_done = rt.sem("exp_done")
            step = rt.sem("step")
            weights_done = rt.sem("weights_done")
            turned = rt.sem("turned")
            cT_hi = rt.sem("cT_hi")
            cT_lo = rt.sem("cT_lo")
            mapped = rt.sem("mapped")
            kept = rt.sem("kept")
            block = rt.block()

            @block.sync
            def _(sp):
                sp.dma_start(gw[:], w["gate_w"]).then_inc(loaded, 16)
                sp.dma_start(sel[:], w["sel"]).then_inc(loaded, 16)
                if biased:
                    sp.dma_start(gb[:], w["gate_b"]).then_inc(loaded, 16)

            @block.scalar
            def _(act):
                act.wait_ge(loaded, 48 if biased else 32)
                act.activation(gwh[:], gw[:], ACT.Copy).then_inc(hi_done, 1)
                act.activation(selr[:], sel[:], ACT.Copy).then_inc(hi_done, 1)
                for c in range(T // CH):
                    act.wait_ge(lgT_done, c + 1)
                    act.activation(lgT[:, c * CH:(c + 1) * CH], wide_ps[0:nr, c, :], ACT.Copy).then_inc(lgT_kept, 1)
                act.wait_ge(shifted, 1)
                act.activation(ex[:], sh[:], ACT.Exp).then_inc(exp_done, 1)
                if shared_gate:
                    act.activation(sg[:], lg[:, :, ne], ACT.Exp, scale=-1.0).then_inc(exp_done, 1)
                for c in range(T // CH):
                    act.wait_ge(turned, c + 1)
                    act.activation(cTh[:, c * CH:(c + 1) * CH], turn_ps[:, c % 2, :], ACT.Copy).then_inc(cT_hi, 1)
                for c in range(T // CH):
                    for m in range(nmap):
                        act.wait_ge(mapped, c * nmap + m + 1)
                        act.activation(cmap[:, m, c * CH:(c + 1) * CH], map_ps[:, (c * nmap + m) % 2, :],
                                       ACT.Copy).then_inc(kept, 1)

            @block.vector
            def _(dve):
                n = [0]

                def chain(i):
                    i.then_inc(step, 1)
                    n[0] += 1
                    dve.wait_ge(step, n[0])

                def spread(a, width):
                    return a[:].unsqueeze(2).to_broadcast([P, NTOK, width])

                dve.wait_ge(loaded, 48 if biased else 32)
                dve.wait_ge(hi_done, 1)
                dve.tensor_tensor(gwl[:], gw[:], gwh[:].bitcast(F32), ALU.subtract).then_inc(lo_done, 1)
                dve.wait_ge(logits_done, 1)
                chain(dve.tensor_copy(lg[:], lg_ps))
                chain(dve.tensor_reduce(mx[:], lg[:, :, 0:ne], AX.X, ALU.max))
                dve.tensor_tensor(sh[:], lg[:, :, 0:ne], spread(mx, ne), ALU.subtract).then_inc(shifted, 1)
                dve.wait_ge(exp_done, 1)
                chain(dve.tensor_reduce(sm[:], ex[:], AX.X, ALU.add))
                chain(dve.reciprocal(sm[:], sm[:]))
                chain(dve.tensor_tensor(pr[:], ex[:], spread(sm, ne), ALU.mult))
                if biased:
                    chain(dve.tensor_tensor(bi[:], pr[:], gb[:].unsqueeze(1).to_broadcast([P, NTOK, ne]), ALU.add))
                else:
                    chain(dve.tensor_copy(bi[:], pr[:]))
                for t in range(NTOK):
                    i = dve.max(top[:, t, :], bi[:, t, :])
                chain(i)
                chain(dve.memset(top[:, :, topk:8], 3.0e38))
                for t in range(NTOK):
                    i = dve.match_replace(rest[:, t, :], top[:, t, :], bi[:, t, :], -3.0e38)
                chain(i)
                chain(dve.tensor_tensor(rest[:], rest[:], bi[:], ALU.not_equal))
                if shared_gate:
                    chain(dve.tensor_tensor(pr[:], pr[:], rest[:], ALU.mult))
                    chain(dve.tensor_reduce(sm[:], pr[:], AX.X, ALU.add))
                    chain(dve.reciprocal(sm[:], sm[:]))
                    chain(dve.tensor_tensor(cw[:, :, 0:ne], pr[:], spread(sm, ne), ALU.mult))
                    dve.wait_ge(exp_done, 2)
                    chain(dve.tensor_scalar(sg[:], sg[:], 1.0, None, ALU.add))
                    dve.reciprocal(cw[:, :, ne], sg[:]).then_inc(weights_done, 1)
                else:
                    chain(dve.memset(cw[:, :, ne:ne + 1], 1.0))
                    dve.tensor_tensor(cw[:, :, 0:ne], pr[:], rest[:], ALU.mult).then_inc(weights_done, 1)
                for c in range(T // CH):
                    dve.wait_ge(cT_hi, c + 1)
                    t = slice(c * CH, (c + 1) * CH)
                    dve.tensor_tensor(cTl[:, t], turn_ps[:, c % 2, :], cTh[:, t].bitcast(F32), ALU.subtract).then_inc(cT_lo, 1)

            @block.tensor
            def _(pe):
                pe.wait_ge(lo_done, 1)
                for c in range(T // CH):
                    for dt in range(DT):
                        i = mm3(pe, wide_ps[0:nr, c, :], gwh[:, dt, :], gwl[:, dt, :], xh[:, dt, c * CH:(c + 1) * CH],
                                xl[:, dt, c * CH:(c + 1) * CH], dt == 0, dt == DT - 1)
                    i.then_inc(lgT_done, 1)
                for t in range(NTOK):
                    if t % (CH // P) == 0:
                        pe.wait_ge(lgT_kept, t * P // CH + 1)
                    i = pe.transpose(lg_ps[:, t, :], lgT[:, t * P:(t + 1) * P], ident[0:nr, 0:nr])
                i.then_inc(logits_done, 1)
                pe.wait_ge(weights_done, 1)
                for c in range(T // CH):
                    if c >= 2:
                        pe.wait_ge(cT_lo, c - 1)
                    for q in range(CH // P):
                        i = pe.transpose(turn_ps[:, c % 2, q * P:(q + 1) * P], cw[:, c * (CH // P) + q, :], ident[:])
                    i.then_inc(turned, 1)
                pe.wait_ge(hi_done, 2)
                for c in range(T // CH):
                    pe.wait_ge(cT_lo, c + 1)
                    for m in range(nmap):
                        k = c * nmap + m
                        if k >= 2:
                            pe.wait_ge(kept, k - 1)
                        t = slice(c * CH, (c + 1) * CH)
                        pe.matmul(map_ps[:, k % 2, :], selr[:, m, :], cTh[:, t], start=True, stop=False)
                        pe.matmul(map_ps[:, k % 2, :], selr[:, m, :], cTl[:, t], start=False, stop=True).then_inc(mapped, 1)

        raw_gu = ph.sb("raw_gu", [P, 2, 2 * DT * P])
        bias = ph.sb("bias", [P, NT, 2])
        bias_now = ph.sb("bias_now", [P, 2, 2])
        hi_gu = ph.sb("hi_gu", [P, 2, 2 * DT * P], F32R)
        lo_gu = ph.sb("lo_gu", [P, 2, 2 * DT * P], F32R)
        raw_dn = ph.sb("raw_dn", [P, 2, D])
        hi_dn = ph.sb("hi_dn", [P, 2, D], F32R)
        lo_dn = ph.sb("lo_dn", [P, 2, D], F32R)
        act_s = ph.sb("act_s", [P, NC, CH])
        hid = ph.sb("hid", [P, NC, CH])
        hid2 = ph.sb("hid2", [P, NC, CH])
        hh = ph.sb("hh", [P, 2, NC, CH], F32R)
        hl = ph.sb("hl", [P, 2, NC, CH], F32R)
        idr = ph.sb("idr", [P, P], F32R)
        if biased:
            b2 = ph.sb("b2", [ne + 1, D])
            b2h = ph.sb("b2h", [ne + 1, D], F32R)
            b2l = ph.sb("b2l", [ne + 1, D], F32R)
            b2_in = ph.sem("b2_in")
            b2_hi = ph.sem("b2_hi")
            b2_lo = ph.sem("b2_lo")
        gate_ps = ph.ps([P, NC, CH])
        up_ps = ph.ps([P, NC, CH])
        y_ps = ph.ps([P, DT, NC, CH])
        raw_gu_in = [ph.sem(f"raw_gu_in{s}") for s in range(2)]
        raw_dn_in = [ph.sem(f"raw_dn_in{s}") for s in range(2)]
        hi_gu_done = ph.sem("hi_gu_done")
        hi_dn_done = ph.sem("hi_dn_done")
        lo_gu_done = ph.sem("lo_gu_done")
        lo_dn_done = ph.sem("lo_dn_done")
        idr_done = ph.sem("idr_done")
        bias_in = ph.sem("bias_in")
        bias_done = ph.sem("bias_done")
        gu_done = ph.sem("gu_done")
        down_done = ph.sem("down_done")
        silu_done = ph.sem("silu_done")
        prod_done = ph.sem("prod_done")
        hid_done = ph.sem("hid_done")
        hhi_done = ph.sem("hhi_done")
        hlo_done = ph.sem("hlo_done")
        y_kept = ph.sem("y_kept")
        block = ph.block()

        segments = [(g * NJ, NJ, g) for g in range(groups)] + [(groups * NJ, nsh, groups if shared_gate else None)]

        def walk(eng, one, begin=None, end=None):
            for half in range(2):
                if begin:
                    begin(half)
                for first, count, m in segments:
                    k0 = half * NT + first
                    peel = count if first == groups * NJ else 3 if count % 2 else 2
                    for i in range(peel):
                        one(k0 + i, (k0 + i) % 2, m, half)
                    if count > peel:
                        with eng.Fori(0, (count - peel) // 2) as it:
                            k1 = it * 2 + (k0 + peel)
                            one(k1, (k0 + peel) % 2, m, half)
                            one(k1 + 1, (k0 + peel + 1) % 2, m, half)
                if end:
                    end(half)

        def known(k, least):
            return not isinstance(k, int) or k >= least

        def load_count(k, slot):
            return 16 * (k // 2 + 1) if isinstance(k, int) else (k + (2 - slot)) * 8

        def tile_of(k, half):
            return k - half * NT

        @block.sync
        def _(sp):
            sp.dma_start(bias[:], w["bias"]).then_inc(bias_in, 16)
            if biased:
                sp.dma_start(b2[:], w["b2"]).then_inc(b2_in, 16)

            def one(k, slot, m, half):
                if known(k, 2):
                    sp.wait_ge(lo_gu_done, k - 1)
                sp.dma_start(raw_gu[:, slot, :], w["gu"][bass.ds(tile_of(k, half), 1), :, :].rearrange("a p n -> p (a n)")).then_inc(raw_gu_in[slot], 16)
                if known(k, 2):
                    sp.wait_ge(lo_dn_done, k - 1)
                sp.dma_start(raw_dn[:, slot, :], w["down"][bass.ds(tile_of(k, half), 1), :, :].rearrange("a p n -> p (a n)")).then_inc(raw_dn_in[slot], 16)

            walk(sp, one)

        @block.gpsimd
        def _(pool):
            def lo_of_gu(k, slot):
                pool.wait_ge(hi_gu_done, k + 1)
                pool.tensor_tensor(lo_gu[:, slot, :], raw_gu[:, slot, :], hi_gu[:, slot, :].bitcast(F32),
                                   ALU.subtract).then_inc(lo_gu_done, 1)

            def one(k, slot, m, half):
                if not isinstance(k, int) or k < 2 * NT - 1:
                    lo_of_gu(k + 1, 1 - slot)
                pool.wait_ge(hi_dn_done, k + 1)
                pool.tensor_tensor(lo_dn[:, slot, :], raw_dn[:, slot, :], hi_dn[:, slot, :].bitcast(F32),
                                   ALU.subtract).then_inc(lo_dn_done, 1)

            lo_of_gu(0, 0)
            walk(pool, one)

        @block.tensor
        def _(pe):
            def begin(half):
                if half == 0:
                    pe.wait_ge(idr_done, 1)
                    if biased:
                        pe.wait_ge(b2_lo, 1)
                else:
                    pe.wait_ge(y_kept, DT * NC)
                for dt in range(DT):
                    for c in range(NC):
                        t0 = half * HALF + c * CH
                        pe.matmul(y_ps[:, dt, c, :], idr[:], xh[:, dt, t0:t0 + CH], start=True, stop=False)
                        pe.matmul(y_ps[:, dt, c, :], idr[:], xl[:, dt, t0:t0 + CH], start=False, stop=False)
                        if biased:
                            d = slice(dt * P, (dt + 1) * P)
                            mm3(pe, y_ps[:, dt, c, :], b2h[:, d], b2l[:, d], cTh[:, t0:t0 + CH], cTl[:, t0:t0 + CH],
                                False, False)

            def down(k, slot, last):
                pe.wait_ge(hlo_done, NC * k + NC)
                pe.wait_ge(lo_dn_done, k + 1)
                for c in range(NC):
                    for dt in range(DT):
                        d0 = dt * P
                        i = mm3(pe, y_ps[:, dt, c, :], hi_dn[:, slot, d0:d0 + P], lo_dn[:, slot, d0:d0 + P],
                                hh[:, slot, c, :], hl[:, slot, c, :], False, last)
                i.then_inc(down_done, 1)

            def one(k, slot, m, half):
                pe.wait_ge(lo_gu_done, k + 1)
                for c in range(NC):
                    t0 = half * HALF + c * CH
                    if known(k, 1):
                        pe.wait_ge(silu_done, NC * (k - 1) + c + 1)
                        pe.wait_ge(prod_done, NC * (k - 1) + c + 1)
                    for side, dst in enumerate((gate_ps, up_ps)):
                        for dt in range(DT):
                            w0 = (side * DT + dt) * P
                            i = mm3(pe, dst[:, c, :], hi_gu[:, slot, w0:w0 + P], lo_gu[:, slot, w0:w0 + P],
                                    xh[:, dt, t0:t0 + CH], xl[:, dt, t0:t0 + CH], dt == 0, dt == DT - 1)
                    i.then_inc(gu_done, 1)
                if not isinstance(k, int) or k % NT > 0:
                    down(k - 1, 1 - slot, False)

            walk(pe, one, begin, lambda half: down((half + 1) * NT - 1, ((half + 1) * NT - 1) % 2, True))

        @block.scalar
        def _(act):
            act.activation(idr[:], ident[:], ACT.Copy).then_inc(idr_done, 1)

            def round_gu(k, slot):
                act.wait_ge(raw_gu_in[slot], load_count(k, slot))
                if known(k, 2):
                    act.wait_ge(gu_done, NC * (k - 1))
                act.activation(hi_gu[:, slot, :], raw_gu[:, slot, :], ACT.Copy).then_inc(hi_gu_done, 1)

            def round_dn(k, slot):
                act.wait_ge(raw_dn_in[slot], load_count(k, slot))
                if known(k, 2):
                    act.wait_ge(down_done, k - 1)
                act.activation(hi_dn[:, slot, :], raw_dn[:, slot, :], ACT.Copy).then_inc(hi_dn_done, 1)

            round_gu(0, 0)
            if biased:
                act.wait_ge(b2_in, 16)
                act.activation(b2h[:], b2[:], ACT.Copy).then_inc(b2_hi, 1)

            def one(k, slot, m, half):
                if not isinstance(k, int) or k < 2 * NT - 1:
                    round_gu(k + 1, 1 - slot)
                act.wait_ge(bias_done, k + 1)
                for c in range(NC):
                    act.wait_ge(gu_done, NC * k + c + 1)
                    if known(k, 1):
                        act.wait_ge(prod_done, NC * (k - 1) + c + 1)
                    act.activation(act_s[:, c, :], gate_ps[:, c, :], ACT.Silu,
                                   bias=bias_now[:, slot, 0:1]).then_inc(silu_done, 1)
                round_dn(k, slot)
                for c in range(NC):
                    if m is None:
                        act.wait_ge(prod_done, NC * k + c + 1)
                    else:
                        act.wait_ge(hid_done, NC * (k - half * unmapped) + c + 1)
                    if known(k, 2) and c == 0:
                        act.wait_ge(down_done, k - 1)
                    act.activation(hh[:, slot, c, :], (hid if m is None else hid2)[:, c, :], ACT.Copy).then_inc(hhi_done, 1)

            def end(half):
                act.wait_ge(down_done, (half + 1) * NT)
                for dt in range(DT):
                    for c in range(NC):
                        t0 = half * HALF + c * CH
                        act.activation(yT[:, dt, t0:t0 + CH], y_ps[:, dt, c, :], ACT.Copy).then_inc(y_kept, 1)

            walk(act, one, None, end)

        @block.vector
        def _(dve):
            def take_bias(tile, slot):
                dve.tensor_scalar(bias_now[:, slot, :], bias[:, tile, :], 0.0, None, ALU.add).then_inc(bias_done, 1)

            def one(k, slot, m, half):
                if not isinstance(k, int):
                    take_bias(bass.ds(k - half * NT + 1, 1), 1 - slot)
                elif k < 2 * NT - 1:
                    take_bias((k + 1) % NT, 1 - slot)
                dve.wait_ge(bias_done, k + 1)
                for c in range(NC):
                    t0 = half * HALF + c * CH
                    dve.wait_ge(silu_done, NC * k + c + 1)
                    if known(k, 1):
                        dve.wait_ge(hlo_done, NC * (k - 1) + c + 1)
                    i = dve.scalar_tensor_tensor(out=hid[:, c, :], in0=up_ps[:, c, :],
                                                 scalar=bias_now[:, slot, 1:2],
                                                 in1=act_s[:, c, :], op0=ALU.add, op1=ALU.mult)
                    i.then_inc(prod_done, 1)
                    dve.wait_ge(prod_done, NC * k + c + 1)
                    if m is not None:
                        dve.tensor_tensor(hid2[:, c, :], hid[:, c, :], cmap[:, m, t0:t0 + CH], ALU.mult).then_inc(hid_done, 1)
                for c in range(NC):
                    dve.wait_ge(hhi_done, NC * k + c + 1)
                    dve.tensor_tensor(hl[:, slot, c, :], (hid if m is None else hid2)[:, c, :], hh[:, slot, c, :].bitcast(F32),
                                      ALU.subtract).then_inc(hlo_done, 1)

            dve.wait_ge(bias_in, 16)
            take_bias(0, 0)
            if biased:
                dve.wait_ge(b2_hi, 1)
                dve.tensor_tensor(b2l[:], b2[:], b2h[:].bitcast(F32), ALU.subtract).then_inc(b2_lo, 1)
            walk(dve, one)


def grouped_attention(nc, tag, a, xh, xl, yT, ident, psum):
    MROW = 64
    NCH = S // CH
    NQ = CH // P
    NK = S // P
    NP = NK // 2
    QUADS = H1 // G1
    NU = QUADS * NCH
    NS = NK * G1
    NM = NQ * G1 * 2
    NR = 3
    ORDER = ("s0t1", "s0tv1")
    W = KV1 // G1 * 2

    with Phase(nc, tag, psum) as ph:
        qd = [nc.dram_tensor(f"{tag}_qd{s}", (D + KV1, T), F32, kind="Internal").ap() for s in range(2)]
        ks = ph.sb("ks", [P, B, G1, S], F32R)
        vs = ph.sb("vs", [P, NTOK, G1, W])
        qm = ph.sb("qm", [P, NCH, G1, CH], F32R)
        qt = ph.sb("qt", [P, NCH, G1, CH], F32R)
        z = ph.sb("z", [P, NTOK, D])

        with Phase(nc, tag + "p", psum) as pj:
            wr = pj.sb("wr", [P, DT, 3 * P])
            wh = pj.sb("wh", [P, DT, 3 * P], F32R)
            wl = pj.sb("wl", [P, DT, 3 * P], F32R)
            bias = pj.sb("bias", [P, 3])
            hi = pj.sb("hi", [P, 3, T], F32R)
            lo = pj.sb("lo", [P, 3, T], F32R)
            kv = pj.sb("kv", [P, T])
            proj_ps = pj.ps([P, 4, CH])
            v_ps = pj.ps([P, 2, CH])
            w_in = pj.sem("w_in")
            wh_done = pj.sem("wh_done")
            wl_done = pj.sem("wl_done")
            cleared = pj.sem("cleared")
            proj_done = pj.sem("proj_done")
            hi_done = pj.sem("hi_done")
            lo_done = pj.sem("lo_done")
            kv_done = pj.sem("kv_done")
            v_turned = pj.sem("v_turned")
            v_kept = pj.sem("v_kept")
            q_out = pj.sem("q_out")
            k_out = [pj.sem(f"k_out{b}") for b in range(B)]
            k_in = pj.sem("k_in")
            NCT = T // CH
            block = pj.block()

            @block.sync
            def _(sp):
                sp.dma_start(wr[:], a["wqkv1"]).then_inc(w_in, 16)
                sp.dma_start(bias[:], a["bqkv1"]).then_inc(w_in, 16)
                for b in range(B):
                    sp.wait_ge(lo_done, (b + 1) * S // CH)
                    for src, dst in ((hi, qd[0]), (lo, qd[1])):
                        sp.dma_start(dst[D:D + KV1, b * S:(b + 1) * S],
                                     src[0:KV1, 2, b * S:(b + 1) * S].bitcast(F32)).then_inc(k_out[b], 16)
                sp.wait_ge(cleared, 3)
                for b in range(B):
                    sp.wait_ge(k_out[b], 32)
                    for r, src in enumerate((qd[0], qd[1], qd[0])):
                        sp.dma_start(ks[r * HD1:(r + 1) * HD1, b, :, :].bitcast(F32),
                                     src[D:D + KV1, b * S:(b + 1) * S].rearrange("(g p) t -> p g t", p=HD1)).then_inc(k_in, 16)
                for m in range(2):
                    sp.wait_ge(lo_done, NCT * (m + 2))
                    for src, dst in ((hi, qd[0]), (lo, qd[1])):
                        sp.dma_start(dst[m * P:(m + 1) * P, :], src[:, m, :].bitcast(F32)).then_inc(q_out, 16)
                sp.wait_ge(k_in, 16 * B * 3)
                sp.wait_ge(q_out, 64)

            @block.gpsimd
            def _(pool):
                pool.memset(ks[:].bitcast(F32), 0.0).then_inc(cleared, 1)
                pool.wait_ge(cleared, 1)
                pool.memset(ks[MROW:MROW + 1, :, :, :].bitcast(F32), 1.0).then_inc(cleared, 1)
                pool.wait_ge(cleared, 2)
                pool.memset(vs[:], 0.0).then_inc(cleared, 1)
                pool.wait_ge(cleared, 3)
                pool.memset(vs[:, :, :, HD1:HD1 + 1], 1.0).then_inc(cleared, 1)
                for t in (qm, qt):
                    pool.memset(t[:].bitcast(F32), 0.0).then_inc(cleared, 1)
                pool.wait_ge(cleared, 6)

            @block.tensor
            def _(pe):
                pe.wait_ge(wl_done, 1)
                for n, m in enumerate((2, 0, 1)):
                    for c in range(NCT):
                        k = n * NCT + c
                        if k >= 4:
                            pe.wait_ge(lo_done, k - 3)
                            if n == 1:
                                pe.wait_ge(kv_done, c + 1)
                        for dt in range(DT):
                            i = mm3(pe, proj_ps[:, k % 4, :], wh[:, dt, m * P:(m + 1) * P], wl[:, dt, m * P:(m + 1) * P],
                                    xh[:, dt, c * CH:(c + 1) * CH], xl[:, dt, c * CH:(c + 1) * CH], dt == 0, dt == DT - 1)
                        i.then_inc(proj_done, 1)
                for c in range(NCT):
                    pe.wait_ge(kv_done, c + 1)
                    if c >= 2:
                        pe.wait_ge(v_kept, c - 1)
                    for q in range(NQ):
                        t0 = c * CH + q * P
                        i = pe.transpose(v_ps[:, c % 2, q * P:(q + 1) * P], kv[:, t0:t0 + P], ident[:])
                    i.then_inc(v_turned, 1)

            @block.scalar
            def _(act):
                act.wait_ge(w_in, 32)
                act.activation(wh[:], wr[:], ACT.Copy).then_inc(wh_done, 1)
                for n, m in enumerate((2, 0, 1)):
                    for c in range(NCT):
                        k = n * NCT + c
                        act.wait_ge(proj_done, k + 1)
                        if n == 0:
                            act.activation(kv[:, c * CH:(c + 1) * CH], proj_ps[:, k % 4, :], ACT.Identity,
                                           bias=bias[:, m:m + 1]).then_inc(kv_done, 1)
                        act.activation(hi[:, m, c * CH:(c + 1) * CH], proj_ps[:, k % 4, :], ACT.Identity,
                                       bias=bias[:, m:m + 1]).then_inc(hi_done, 1)

            @block.vector
            def _(dve):
                dve.wait_ge(wh_done, 1)
                dve.tensor_tensor(wl[:], wr[:], wh[:].bitcast(F32), ALU.subtract).then_inc(wl_done, 1)
                for n, m in enumerate((2, 0, 1)):
                    for c in range(NCT):
                        k = n * NCT + c
                        dve.wait_ge(hi_done, k + 1)
                        dve.scalar_tensor_tensor(out=lo[:, m, c * CH:(c + 1) * CH], in0=proj_ps[:, k % 4, :],
                                                 scalar=bias[:, m:m + 1], in1=hi[:, m, c * CH:(c + 1) * CH].bitcast(F32),
                                                 op0=ALU.add, op1=ALU.subtract).then_inc(lo_done, 1)
                dve.wait_ge(cleared, 4)
                for c in range(NCT):
                    dve.wait_ge(v_turned, c + 1)
                    dve.tensor_copy(vs[:, c * NQ:(c + 1) * NQ, :, 0:HD1],
                                    v_ps[:, c % 2, :].rearrange("p (q n) -> p q n", n=P)[:, :, KV1:2 * KV1]
                                    .rearrange("p q (g e) -> p q g e", e=HD1)).then_inc(v_kept, 1)

        with Phase(nc, tag + "m", psum) as am:
            pt = am.sb("pt", [P, 2, G1, 2, CH])
            part = am.sb("part", [P, 2, NQ, G1, 2])
            negm = am.sb("negm", [P, 2, NQ * G1])
            mrow = am.sb("mrow", [NQ * G1, P], F32R)
            zt = am.sb("zt", [P, CH])
            rden = am.sb("rden", [P, NQ, G1])
            st_ps = am.ps([P, NR, CH])
            mx_ps = am.ps([P, NR, CH])
            acc_ps = am.ps([P, CH])
            misc_ps = am.ps([P, CH])
            qm_in = [am.sem(f"qm_in{s}") for s in range(2)]
            qt_in = [am.sem(f"qt_in{s}") for s in range(2)]
            m_in = [am.sem(f"m_in{s}") for s in range(2)]
            mx_ready = am.sem("mx_ready")
            mx_taken = am.sem("mx_taken")
            negm_done = am.sem("negm_done")
            m_turned = am.sem("m_turned")
            m_kept = am.sem("m_kept")
            st_ready = am.sem("st_ready")
            exp_done = am.sem("exp_done")
            pv_done = am.sem("pv_done")
            zt_done = am.sem("zt_done")
            z_turned = am.sem("z_turned")
            rden_done = am.sem("rden_done")
            z_done = am.sem("z_done")
            block = am.block()

            def walk(eng, quad, begin=None):
                if begin:
                    begin()
                for b in range(B):
                    quad(lambda c: b if c >= 0 else b - 1, 0, b * NU, b == 0, False)
                    with eng.Fori(1, QUADS - 1) as j:
                        quad(lambda c: b, j, j * NCH + b * NU, False, False)
                    quad(lambda c: b if c < NCH else b + 1, QUADS - 1, b * NU + (QUADS - 1) * NCH, False, b == B - 1)

            def bank(i):
                return i % NR

            def back(i):
                return 1 if i == 0 else NR

            def place(c, kp, g, k):
                return c * NS + (kp * G1 + g) * 2 + k

            def first_of_all(u, least):
                return isinstance(u, int) and u < least

            @block.sync
            def _(sp):
                def fetch(dst, sem, b, j, c):
                    for r, src in enumerate((qd[0], qd[0], qd[1])):
                        rows = src[bass.ds(j * (G1 * HD1), G1 * HD1), b * S + c * CH:b * S + (c + 1) * CH]
                        sp.dma_start(dst[r * HD1:(r + 1) * HD1, c, :, :].bitcast(F32),
                                     rows.rearrange("(g p) t -> p g t", p=HD1)).then_inc(sem[c], 16)

                def quad(at, j, u0, first, last):
                    b = at(0)
                    for c in range(NCH):
                        u = u0 + c
                        if not first_of_all(u, 2):
                            sp.wait_ge(mx_ready, (u - 1) * NM)
                        fetch(qm, qm_in, b, j, c)
                        if not first_of_all(u, 2):
                            sp.wait_ge(st_ready, (u - 1) * NS)
                        fetch(qt, qt_in, b, j, c)

                walk(sp, quad)

            def dma_count(u, c, each):
                return (u // 2 + 1) * 16 * each if isinstance(u, int) else (u + (2 - c)) * (8 * each)

            @block.tensor
            def _(pe):
                def maxima(b, u, c, q, g, half, i):
                    if q == 0 and g == 0 and half == 0:
                        pe.wait_ge(qm_in[c], dma_count(u, c, 3))
                    n = u * NM + ((q * G1 + g) * 2 + half)
                    if not first_of_all(n, back(i)):
                        pe.wait_ge(mx_taken, n - (back(i) - 1))
                    pe.matmul(mx_ps[:, bank(i), :], qm[:, c, g, q * P:(q + 1) * P],
                              ks[:, b, g, half * CH:(half + 1) * CH], start=True, stop=True).then_inc(mx_ready, 1)

                def turn_maxima(u, c, behind=2):
                    pe.wait_ge(negm_done, u + 1)
                    if not first_of_all(u, behind + 1):
                        pe.wait_ge(z_done, u - behind)
                    pe.transpose(misc_ps[0:NQ * G1, 0:P], negm[:, c, :], ident[:]).then_inc(m_turned, 1)

                def scores(b, u, c, kp, g, k):
                    if kp == 0 and g == 0 and k == 0:
                        pe.wait_ge(qt_in[c], dma_count(u, c, 3))
                        pe.wait_ge(m_in[c], dma_count(u, c, G1))
                    i = place(c, kp, g, k)
                    n = u * NS + ((kp * G1 + g) * 2 + k)
                    if not first_of_all(n, back(i)):
                        pe.wait_ge(exp_done, n - (back(i) - 1))
                    kt = kp * 2 + k
                    pe.matmul(st_ps[:, bank(i), :], ks[:, b, g, kt * P:(kt + 1) * P], qt[:, c, g, :],
                              start=True, stop=True).then_inc(st_ready, 1)

                def values(b, u, kp, k):
                    if k == 0:
                        pe.wait_ge(exp_done, u * NS + (kp + 1) * (G1 * 2))
                        if kp == 0 and not first_of_all(u, 1):
                            pe.wait_ge(zt_done, u)
                    kt = kp * 2 + k
                    for g in range(G1):
                        i = pe.matmul(acc_ps[g * W:(g + 1) * W, :], vs[:, b * NK + kt, g, :], pt[:, kp % 2, g, k, :],
                                      start=kt == 0, stop=kt == NK - 1, tile_position=(0, g * W))
                    if k == 1:
                        i.then_inc(pv_done, 1)

                def turn_z(u, ahead):
                    pe.wait_ge(zt_done, u + 1)
                    pe.wait_ge(m_kept, u + ahead)
                    if ahead == 2:
                        pe.wait_ge(z_done, u)
                    for q in range(NQ):
                        i = pe.transpose(misc_ps[:, q * P:(q + 1) * P], zt[:, q * P:(q + 1) * P], ident[:])
                    i.then_inc(z_turned, 1)

                def begin():
                    for n in range(NQ * G1 * 2):
                        maxima(0, 0, 0, n // (G1 * 2), n // 2 % G1, n % 2, n)
                    turn_maxima(0, 0, 0)
                    for n in range(NQ // 2 * G1 * 2):
                        maxima(0, 1, 1, n // (G1 * 2), n // 2 % G1, n % 2, NM + n)

                def quad(at, j, u0, first, last):
                    for c in range(NCH):
                        u = u0 + c
                        for kp in range(NP):
                            for g in range(G1):
                                for step in ORDER[g % 2]:
                                    if step in "st":
                                        scores(at(c), u, c, kp, g, "st".index(step))
                                    elif step == "v":
                                        if kp > 0:
                                            values(at(c), u, kp - 1, g // 2)
                                        elif not (first and c == 0):
                                            values(at(c - 1), u - 1, NP - 1, g // 2)
                                    elif kp < 2 and not (last and c == 1):
                                        maxima(at(c + 1), u + 1, 1 - c, kp + 2, g, int(step), place(c, kp, g, int(step)))
                                    elif kp >= 2 and not last:
                                        maxima(at(c + 2), u + 2, c, kp - 2, g, int(step), place(c, kp, g, int(step)))
                            if kp == 2 and not (last and c == 1):
                                turn_maxima(u + 1, 1 - c)
                            if kp == 3 and not (first and c == 0):
                                turn_z(u - 1, 2 if last and c == 1 else 3)
                    if last:
                        for k in range(2):
                            values(at(1), u, NP - 1, k)
                        pe.wait_ge(zt_done, u + 1)
                        pe.wait_ge(z_done, u)
                        for q in range(NQ):
                            i = pe.transpose(misc_ps[:, q * P:(q + 1) * P], zt[:, q * P:(q + 1) * P], ident[:])
                        i.then_inc(z_turned, 1)

                walk(pe, quad, begin)

            @block.scalar
            def _(act):
                def keep_maxima(u, c):
                    act.wait_ge(m_turned, u + 1)
                    if not first_of_all(u, 1):
                        act.wait_ge(m_in[1 - c], dma_count(u - 1, 1 - c, G1))
                    act.activation(mrow[:], misc_ps[0:NQ * G1, 0:P], ACT.Copy).then_inc(m_kept, 1)

                def send_maxima(u, c):
                    act.wait_ge(m_kept, u + 1)
                    if not first_of_all(u, 2):
                        act.wait_ge(st_ready, (u - 1) * NS)
                    for g in range(G1):
                        act.dma_start(qt[MROW:MROW + 1, c, g, :].bitcast(F32),
                                      mrow[g * NQ:(g + 1) * NQ, :].bitcast(F32)).then_inc(m_in[c], 16)

                def keep_z(u):
                    act.wait_ge(pv_done, (u + 1) * NP)
                    if not first_of_all(u, 1):
                        act.wait_ge(z_turned, u)
                    act.activation(zt[:], acc_ps[:], ACT.Copy).then_inc(zt_done, 1)

                def quad(at, j, u0, first, last):
                    for c in range(NCH):
                        u = u0 + c
                        for kp in range(NP):
                            for g in range(G1):
                                for k in range(2):
                                    act.wait_ge(st_ready, u * NS + ((kp * G1 + g) * 2 + k + 1))
                                    s = u * NP + kp
                                    if g == 0 and k == 0 and not first_of_all(s, 2):
                                        act.wait_ge(pv_done, s - 1)
                                    act.activation(pt[:, kp % 2, g, k, :], st_ps[:, bank(place(c, kp, g, k)), :], ACT.Exp,
                                                   scale=1.0 / HD1).then_inc(exp_done, 1)
                                if kp == 3 and g == 0 and not (last and c == 1):
                                    send_maxima(u + 1, 1 - c)
                            if kp == 0 and not (first and c == 0):
                                keep_z(u - 1)
                            if kp == 2 and not (last and c == 1):
                                keep_maxima(u + 1, 1 - c)
                    if last:
                        keep_z(u)

                def begin():
                    keep_maxima(0, 0)
                    send_maxima(0, 0)

                walk(act, quad, begin)

            @block.vector
            def _(dve):
                def maxima(u, c, q, at):
                    for g in range(G1):
                        for half in range(2):
                            n = u * NM + ((q * G1 + g) * 2 + half)
                            dve.wait_ge(mx_ready, n + 1)
                            if q == 0 and g == 0 and half == 0 and not first_of_all(u, 2):
                                dve.wait_ge(negm_done, u - 1)
                            dve.tensor_reduce(part[:, c, q, g, half:half + 1], mx_ps[:, bank(at + g * 2 + half), :], AX.X,
                                              ALU.max).then_inc(mx_taken, 1)
                    if q == NQ - 1:
                        dve.wait_ge(mx_taken, (u + 1) * NM)
                        if not first_of_all(u, 2):
                            dve.wait_ge(m_turned, u - 1)
                        dve.tensor_reduce(negm[:, c, :].rearrange("p (g q) -> p q g", q=NQ), part[:, c, :, :, :], AX.X,
                                          ALU.max, negate=True).then_inc(negm_done, 1)

                def keep_z(b, j, u, c):
                    dve.wait_ge(z_turned, u + 1)
                    if not first_of_all(u, 1):
                        dve.wait_ge(z_done, u)
                    src = misc_ps[:].rearrange("p (q g e) -> p q g e", g=G1, e=W)
                    dve.reciprocal(rden[:], src[:, :, :, HD1]).then_inc(rden_done, 1)
                    dve.wait_ge(rden_done, u + 1)
                    t0 = b * NK + c * NQ
                    dst = z[:, t0:t0 + NQ, bass.ds(j * (G1 * HD1), G1 * HD1)].rearrange("p q (g e) -> p q g e", e=HD1)
                    dve.tensor_tensor(dst, src[:, :, :, 0:HD1],
                                      rden[:].unsqueeze(3).to_broadcast([P, NQ, G1, HD1]), ALU.mult).then_inc(z_done, 1)

                def begin():
                    for q in range(NQ):
                        maxima(0, 0, q, place(0, q, 0, 0))
                    for q in range(NQ // 2):
                        maxima(1, 1, q, place(1, q, 0, 0))

                def quad(at, j, u0, first, last):
                    for c in range(NCH):
                        u = u0 + c
                        for kp in range(NP):
                            if kp < 2 and not (last and c == 1):
                                maxima(u + 1, 1 - c, kp + 2, place(c, kp, 0, 0))
                            if kp >= 2 and not last:
                                maxima(u + 2, c, kp - 2, place(c, kp, 0, 0))
                            if kp == 3 and not (first and c == 0):
                                keep_z(at(c - 1), j if c else QUADS - 1 if at(-1) < at(0) else j - 1, u - 1, 1 - c)
                    if last:
                        keep_z(at(1), j, u, 1)

                walk(dve, quad, begin)

        with Phase(nc, tag + "o", psum) as op:
            wr = op.sb("wr", [P, DT, D])
            wh = op.sb("wh", [P, DT, D], F32R)
            wl = op.sb("wl", [P, DT, D], F32R)
            bias = op.sb("bias", [P, DT])
            zh = op.sb("zh", [P, DT, T], F32R)
            zl = op.sb("zl", [P, DT, T], F32R)
            idr = op.sb("idr", [P, P], F32R)
            turn_ps = op.ps([P, 4, CH])
            out_ps = op.ps([P, 4, CH])
            w_in = op.sem("w_in")
            wh_done = op.sem("wh_done")
            wl_done = op.sem("wl_done")
            turned = op.sem("turned")
            hi_done = op.sem("hi_done")
            lo_done = op.sem("lo_done")
            out_done = op.sem("out_done")
            y_done = op.sem("y_done")
            NCT = T // CH
            block = op.block()

            @block.sync
            def _(sp):
                sp.dma_start(wr[:], a["wo1"]).then_inc(w_in, 16)
                sp.dma_start(bias[:], a["bo1"]).then_inc(w_in, 16)

            @block.tensor
            def _(pe):
                def turn(c):
                    for dt in range(DT):
                        k = c * DT + dt
                        if k >= 4:
                            pe.wait_ge(lo_done, k - 3)
                        for q in range(NQ):
                            i = pe.transpose(turn_ps[:, k % 4, q * P:(q + 1) * P], z[:, c * NQ + q, dt * P:(dt + 1) * P], ident[:])
                        i.then_inc(turned, 1)

                turn(0)
                pe.wait_ge(wl_done, 1)
                for c in range(NCT):
                    if c + 1 < NCT:
                        turn(c + 1)
                    pe.wait_ge(lo_done, DT * (c + 1))
                    for m in range(DT):
                        k = c * DT + m
                        if k >= 4:
                            pe.wait_ge(y_done, k - 3)
                        o = out_ps[:, k % 4, :]
                        t = slice(c * CH, (c + 1) * CH)
                        pe.matmul(o, idr[:], xh[:, m, t], start=True, stop=False)
                        pe.matmul(o, idr[:], xl[:, m, t], start=False, stop=False)
                        for dt in range(DT):
                            i = mm3(pe, o, wh[:, dt, m * P:(m + 1) * P], wl[:, dt, m * P:(m + 1) * P],
                                    zh[:, dt, t], zl[:, dt, t], False, dt == DT - 1)
                        i.then_inc(out_done, 1)

            @block.scalar
            def _(act):
                act.wait_ge(w_in, 32)
                act.activation(wh[:], wr[:], ACT.Copy).then_inc(wh_done, 1)
                act.activation(idr[:], ident[:], ACT.Copy).then_inc(wh_done, 1)

                def keep(c):
                    for m in range(DT):
                        k = c * DT + m
                        act.wait_ge(out_done, k + 1)
                        act.activation(yT[:, m, c * CH:(c + 1) * CH], out_ps[:, k % 4, :], ACT.Identity,
                                       bias=bias[:, m:m + 1]).then_inc(y_done, 1)

                for c in range(NCT):
                    for dt in range(DT):
                        k = c * DT + dt
                        act.wait_ge(turned, k + 1)
                        act.activation(zh[:, dt, c * CH:(c + 1) * CH], turn_ps[:, k % 4, :], ACT.Copy).then_inc(hi_done, 1)
                    if c:
                        keep(c - 1)
                keep(NCT - 1)

            @block.vector
            def _(dve):
                dve.wait_ge(wh_done, 2)
                dve.tensor_tensor(wl[:], wr[:], wh[:].bitcast(F32), ALU.subtract).then_inc(wl_done, 1)
                for c in range(NCT):
                    for dt in range(DT):
                        k = c * DT + dt
                        dve.wait_ge(hi_done, k + 1)
                        dve.tensor_tensor(zl[:, dt, c * CH:(c + 1) * CH], turn_ps[:, k % 4, :],
                                          zh[:, dt, c * CH:(c + 1) * CH].bitcast(F32), ALU.subtract).then_inc(lo_done, 1)


def causal_attention(nc, tag, a, xh, xl, yT, ident, psum):
    NQ = S // P
    HB = 2 * H0
    CQ = CH // P
    SCALE = float(E0) ** -0.5
    NP = 4
    MASKED = -1.0e30
    PLAN = [[("pv", 1, True)],
            [("q", 0), ("k", 0)],
            [("o", 1, True, 0)],
            [("o", 1, True, 1), ("q", 1)],
            [("k", 1), ("vt", 0)],
            [("vt", 1), ("v", 0)],
            [("pv", 0, False), ("v", 1)],
            [("o", 0, False, 0), ("o", 0, False, 1)]]
    PROJECT = ("q", "k", "vt", "v")
    WHOLE = ("o", "vt")

    def plan(first, last):
        def wanted(t):
            return not (first and t[0] in ("pv", "o") and t[2]) and not (last and t[0] in PROJECT)
        return [[t for t in unit if wanted(t)] for unit in PLAN]

    SPLITS = 4
    NTASK = sum(len(u) for u in PLAN)
    NHI = sum(t[0] not in WHOLE for u in PLAN for t in u)
    PRE = [("q", 0), ("k", 0), ("q", 1), ("k", 1), ("vt", 0), ("vt", 1), ("v", 0), ("v", 1)]
    HIPRE = sum(t[0] not in WHOLE for t in PRE)
    TASKS1 = len(PRE) + sum(len(u) for u in plan(True, False))
    HIS1 = HIPRE + sum(t[0] not in WHOLE for u in plan(True, False) for t in u)

    def bases(hb):
        if isinstance(hb, int) and hb == 0:
            return len(PRE), HIPRE
        return (hb - 1) * NTASK + TASKS1, (hb - 1) * NHI + HIS1

    def done_by(hb, task):
        if isinstance(hb, int) and hb == -1:
            return PRE.index(task) + 1
        first = isinstance(hb, int) and hb == 0
        last = isinstance(hb, int) and hb == HB - 1
        flat = [t for u in plan(first, last) for t in u]
        return bases(hb)[0] + flat.index(task) + 1

    def bank_of(b, first, n):
        return ((len(PRE) if first else TASKS1) + n) % 2

    NB = CQ + 2 * (NQ - CQ)

    def batches(qt):
        if qt < CQ:
            return [(0, qt + 1, qt)]
        n = CQ + 2 * (qt - CQ)
        return [(0, CQ, n), (CQ, qt + 1 - CQ, n + 1)]

    with Phase(nc, tag, psum) as ph:
        wr = ph.sb("wr", [P, 2, 3, DT, E0])
        wh = ph.sb("wh", [P, 2, 3, DT, E0], F32R)
        wl = ph.sb("wl", [P, 2, 3, DT, E0], F32R)
        wor = ph.sb("wor", [P, D])
        woh = ph.sb("woh", [P, D], F32R)
        wol = ph.sb("wol", [P, D], F32R)
        qh = ph.sb("qh", [P, B, S], F32R)
        ql = ph.sb("ql", [P, B, S], F32R)
        kh = ph.sb("kh", [P, B, S], F32R)
        kl = ph.sb("kl", [P, B, S], F32R)
        vh = ph.sb("vh", [P, B, NQ, E0], F32R)
        vl = ph.sb("vl", [P, B, NQ, E0], F32R)
        pr = ph.sb("pr", [P, NP, S])
        pth = [ph.sb(f"pth{c}", [P, CQ * (c + 1), CH], F32R) for c in range(2)]
        ptl = [ph.sb(f"ptl{c}", [P, CQ * (c + 1), CH], F32R) for c in range(2)]
        vt = ph.sb("vt", [P, 2, CH])
        zh = ph.sb("zh", [P, 2, CH], F32R)
        zl = ph.sb("zl", [P, 2, CH], F32R)
        negm = ph.sb("negm", [P, NP])
        rsum = ph.sb("rsum", [P, NP])
        rinv = ph.sb("rinv", [P, NP])
        mask0 = ph.sb("mask0", [P, P])
        mask = ph.sb("mask", [P, P], F32R)
        idr = ph.sb("idr", [P, P], F32R)
        s_ps = ph.ps([P, 2, S])
        t_ps = ph.ps([P, 2, CH])
        r_ps = ph.ps([P, 2, CH])
        cleared = ph.sem("cleared")
        mask_set = ph.sem("mask_set")
        rounded = ph.sem("rounded")
        wr_in = [ph.sem(f"wr_in{s}") for s in range(2)]
        wh_done = ph.sem("wh_done")
        wl_done = ph.sem("wl_done")
        wor_in = ph.sem("wor_in")
        woh_done = ph.sem("woh_done")
        wol_done = ph.sem("wol_done")
        s_ready = ph.sem("s_ready")
        max_done = ph.sem("max_done")
        exp_done = ph.sem("exp_done")
        inv_done = ph.sem("inv_done")
        p_done = ph.sem("p_done")
        t_ready = ph.sem("t_ready")
        th_done = ph.sem("th_done")
        tl_done = ph.sem("tl_done")
        task_done = ph.sem("task_done")
        task_hi = ph.sem("task_hi")
        task_out = ph.sem("task_out")
        block = ph.block()

        def walk(eng, half, begin=None, end=None):
            if begin:
                begin()
            half(0, 0, 0, True, False)
            with eng.Fori(0, H0 - 2) as h:
                half(h * 2 + 1, h, 1, False, False)
                half(h * 2 + 2, h + 1, 0, False, False)
            half(HB - 3, H0 - 2, 1, False, False)
            half(HB - 2, H0 - 1, 0, False, False)
            half(HB - 1, H0 - 1, 1, False, True)
            if end:
                end()

        def at_least(n, least):
            return not isinstance(n, int) or n >= least

        def pair_of(task, b):
            kind, c = task[0], task[1]
            t = slice(c * CH, (c + 1) * CH)
            if kind == "q":
                return qh[:, 1 - b, t], ql[:, 1 - b, t]
            if kind == "k":
                return kh[:, 1 - b, t], kl[:, 1 - b, t]
            if kind == "v":
                t = slice(c * CQ, (c + 1) * CQ)
                return (vh[:, 1 - b, t, :].rearrange("p t e -> p (t e)"), vl[:, 1 - b, t, :].rearrange("p t e -> p (t e)"))
            return zh[:, c, :], zl[:, c, :]

        @block.sync
        def _(sp):
            def load(n, s, h):
                if at_least(n, 2):
                    sp.wait_ge(wl_done, (n - 1) * 3)
                sp.dma_start(wr[:, s], a["qkv0"][bass.ds(h, 1)].rearrange("o p w t e -> (o p) w t e")).then_inc(wr_in[s], 16)

            def load_o(h):
                if at_least(h, 1):
                    sp.wait_ge(wol_done, h)
                sp.dma_start(wor[:], a["o0"][bass.ds(h, 1)].rearrange("o e d -> (o e) d")).then_inc(wor_in, 16)

            load(0, 0, 0)
            load(1, 1, 0)
            load_o(0)
            with sp.Fori(1, H0) as h:
                load(h * 2, 0, h)
                load(h * 2 + 1, 1, h)
                load_o(h)

        @block.gpsimd
        def _(pool):
            def split(n, s, w):
                pool.wait_ge(wh_done, n + 1)
                pool.tensor_tensor(wl[:, s, w].rearrange("p t e -> p (t e)"), wr[:, s, w].rearrange("p t e -> p (t e)"),
                                   wh[:, s, w].rearrange("p t e -> p (t e)").bitcast(F32),
                                   ALU.subtract).then_inc(wl_done, 1)

            def split_o(h):
                pool.wait_ge(woh_done, h + 1)
                pool.tensor_tensor(wol[:], wor[:], woh[:].bitcast(F32), ALU.subtract).then_inc(wol_done, 1)

            pool.memset(mask0[:], 0.0).then_inc(cleared, 1)
            pool.wait_ge(cleared, 1)
            pool.affine_select(out=mask0[:], in_=mask0[:], compare_op=ALU.is_ge, fill=MASKED, base=0,
                               pattern=[[-1, P]], channel_multiplier=1).then_inc(mask_set, 1)

            def normalise(hb, qt):
                pool.wait_ge(inv_done, hb * NQ + (qt + 1))
                j, n = qt % NP, (qt + 1) * P
                pool.tensor_tensor(pr[:, j, 0:n], pr[:, j, 0:n], rinv[:, j:j + 1].to_broadcast([P, n]),
                                   ALU.mult).then_inc(p_done, 1)

            def half(hb, h, b, first, last):
                for qt in range(NQ):
                    if qt < NQ - 1:
                        normalise(hb, qt + 1)
                    elif not last:
                        normalise(hb + 1, 0)
                    if SPLITS <= qt < SPLITS + 3 and (not isinstance(hb, int) or hb < HB - 2):
                        split(hb + 2, b, qt - SPLITS)
                    if qt == NQ - 3 and b == 0 and not first:
                        split_o(h)

            def begin():
                for w in range(3):
                    split(0, 0, w)
                normalise(0, 0)
                for w in range(3):
                    split(1, 1, w)
                split_o(0)

            walk(pool, half, begin)

        @block.tensor
        def _(pe):
            def scores(hb, b, qt):
                u = hb * NQ + qt
                if qt == 0:
                    pe.wait_ge(task_out, done_by(hb - 1, ("k", 0)))
                if qt == CQ:
                    pe.wait_ge(task_out, done_by(hb - 1, ("k", 1)))
                if at_least(u, 2):
                    pe.wait_ge(exp_done, u - 1)
                q0 = qt * P
                keys = q0 + P
                for k0 in range(0, keys, CH):
                    k1 = min(keys, k0 + CH)
                    o = s_ps[:, qt % 2, k0:k1]
                    i = mm3(pe, o, qh[:, b, q0:q0 + P], ql[:, b, q0:q0 + P], kh[:, b, k0:k1], kl[:, b, k0:k1],
                            True, k1 < keys)
                i = pe.matmul(s_ps[:, qt % 2, q0:q0 + P], idr[:], mask[:], start=False, stop=True)
                i.then_inc(s_ready, 1)

            def turn(hb, qt):
                pe.wait_ge(p_done, hb * NQ + (qt + 1))
                for k0, count, n in batches(qt):
                    m = hb * NB + n
                    if at_least(m, 2):
                        pe.wait_ge(tl_done, m - 1)
                    for k in range(count):
                        i = pe.transpose(t_ps[:, n % 2, k * P:(k + 1) * P], pr[:, qt % NP, (k0 + k) * P:(k0 + k + 1) * P],
                                         ident[:])
                    i.then_inc(t_ready, 1)

            def task(hb, h, b, t, k, bank):
                if at_least(k, 2):
                    pe.wait_ge(task_out, k - 1)
                o = r_ps[:, bank, :]
                kind, c = t[0], t[1]
                nb = 1 - b
                x0 = nb * S + c * CH
                if kind in ("q", "k", "vt"):
                    if kind == "q" and c == 0:
                        pe.wait_ge(wl_done, (hb + 2) * 3)
                    w = PROJECT.index(kind)
                    for dt in range(DT):
                        i = mm3(pe, o, wh[:, nb, w, dt, :], wl[:, nb, w, dt, :], xh[:, dt, x0:x0 + CH], xl[:, dt, x0:x0 + CH],
                                dt == 0, dt == DT - 1)
                elif kind == "v":
                    pe.wait_ge(task_out, done_by(hb, ("vt", c)))
                    for q in range(CQ):
                        i = pe.transpose(o[:, q * P:(q + 1) * P], vt[:, c, q * P:(q + 1) * P], ident[:])
                elif kind == "pv":
                    hs, vb = (hb - 1, nb) if t[2] else (hb, b)
                    pe.wait_ge(tl_done, hs * NB + (NB if c else CQ))
                    if c == 0:
                        pe.wait_ge(task_out, done_by(hs - 1, ("v", 1)))
                    for kt in range(CQ * (c + 1)):
                        q0 = max(0, kt - CQ * c) * P
                        i = mm3(pe, o[:, q0:CH], vh[:, vb, kt, :], vl[:, vb, kt, :], pth[c][:, kt, q0:CH], ptl[c][:, kt, q0:CH],
                                kt == 0, kt == CQ * (c + 1) - 1)
                else:
                    dt = t[3]
                    if dt == 0:
                        pe.wait_ge(task_out, done_by(hb, ("pv", c, t[2])))
                        if not (t[2]):
                            pe.wait_ge(wol_done, h + 1)
                    i = mm3(pe, o, woh[:, dt * P:(dt + 1) * P], wol[:, dt * P:(dt + 1) * P], zh[:, c, :], zl[:, c, :],
                            True, True)
                i.then_inc(task_done, 1)

            def half(hb, h, b, first, last):
                k, n = bases(hb)[0], 0
                for qt, tasks in enumerate(plan(first, last)):
                    if qt < NQ - 2:
                        scores(hb, b, qt + 2)
                    elif not last:
                        scores(hb + 1, 1 - b, qt + 2 - NQ)
                    turn(hb, qt)
                    for t in tasks:
                        task(hb, h, b, t, k + n, bank_of(b, first, n))
                        n += 1

            def begin():
                pe.wait_ge(rounded, 2)
                for n, t in enumerate(PRE):
                    task(-1, 0, 1, t, n, n % 2)
                for qt in range(2):
                    scores(0, 0, qt)

            def end():
                k = bases(HB - 1)[0] + sum(len(u) for u in plan(False, True))
                for n, t in enumerate([("pv", 1, True), ("o", 1, True, 0), ("o", 1, True, 1)]):
                    if t[0] == "o" and t[3] == 0:
                        pe.wait_ge(task_out, k + 1)
                    finish(t, k + n)

            def finish(t, k):
                pe.wait_ge(task_out, k - 1)
                o = r_ps[:, k % 2, :]
                if t[0] == "pv":
                    pe.wait_ge(tl_done, HB * NB)
                    for kt in range(NQ):
                        q0 = max(0, kt - CQ) * P
                        i = mm3(pe, o[:, q0:CH], vh[:, 1, kt, :], vl[:, 1, kt, :], pth[1][:, kt, q0:CH], ptl[1][:, kt, q0:CH],
                                kt == 0, kt == NQ - 1)
                else:
                    dt = t[3]
                    i = mm3(pe, o, woh[:, dt * P:(dt + 1) * P], wol[:, dt * P:(dt + 1) * P], zh[:, 1, :], zl[:, 1, :],
                            True, True)
                i.then_inc(task_done, 1)

            walk(pe, half, begin, end)

        @block.scalar
        def _(act):
            def soften(hb, qt):
                u = hb * NQ + qt
                act.wait_ge(max_done, u + 1)
                if at_least(u, NP):
                    nb = qt - NP if qt >= NP else qt - NP + NQ
                    hp = hb if qt >= NP else hb - 1
                    act.wait_ge(t_ready, hp * NB + (batches(nb)[-1][2] + 1))
                n = (qt + 1) * P
                act.activation(pr[:, qt % NP, 0:n], s_ps[:, qt % 2, 0:n], ACT.Exp, bias=negm[:, qt % NP:qt % NP + 1],
                               accum_out=rsum[:, qt % NP:qt % NP + 1]).then_inc(exp_done, 1)

            def keep_hi(hb, qt):
                for k0, count, n in batches(qt):
                    act.wait_ge(t_ready, hb * NB + (n + 1))
                    c, q0 = qt // CQ, (qt % CQ) * P
                    act.activation(pth[c][:, k0:k0 + count, q0:q0 + P],
                                   t_ps[:, n % 2, 0:count * P].rearrange("p (k q) -> p k q", q=P), ACT.Copy).then_inc(th_done, 1)

            def round_weights(s, count):
                act.wait_ge(wr_in[s], count)
                act.activation(wh[:, s], wr[:, s], ACT.Copy).then_inc(wh_done, 1)

            def round_o(h):
                act.wait_ge(wor_in, (h + 1) * 16)
                if at_least(h, 1):
                    act.wait_ge(task_done, done_by(h * 2, ("o", 1, True, 1)))
                act.activation(woh[:], wor[:], ACT.Copy).then_inc(woh_done, 1)

            def task(b, t, k, bank):
                act.wait_ge(task_done, k + 1)
                act.activation(pair_of(t, b)[0], r_ps[:, bank, :], ACT.Copy,
                               scale=SCALE if t[0] == "q" else 1.0).then_inc(task_hi, 1)

            def half(hb, h, b, first, last):
                k, n = bases(hb)[0], 0
                for qt, tasks in enumerate(plan(first, last)):
                    keep_hi(hb, qt)
                    if qt < NQ - 2:
                        soften(hb, qt + 2)
                    elif not last:
                        soften(hb + 1, qt + 2 - NQ)
                    for t in tasks:
                        if t[0] not in WHOLE:
                            task(b, t, k + n, bank_of(b, first, n))
                        n += 1
                    if qt == 3:
                        if not isinstance(hb, int) or hb < HB - 2:
                            round_weights(b, (h + 2) * 16)
                        if b == 0 and not first:
                            round_o(h)

            def begin():
                round_weights(0, 16)
                round_weights(1, 16)
                round_o(0)
                act.wait_ge(mask_set, 1)
                act.activation(mask[:], mask0[:], ACT.Copy).then_inc(rounded, 1)
                act.activation(idr[:], ident[:], ACT.Copy).then_inc(rounded, 1)
                for n, t in enumerate(PRE):
                    if t[0] not in WHOLE:
                        task(1, t, n, n % 2)
                for qt in range(2):
                    soften(0, qt)

            def end():
                k = bases(HB - 1)[0] + sum(len(u) for u in plan(False, True))
                task(0, ("pv", 1, True), k, k % 2)

            walk(act, half, begin, end)

        @block.vector
        def _(dve):
            def maximum(hb, qt):
                u = hb * NQ + qt
                dve.wait_ge(s_ready, u + 1)
                n = (qt + 1) * P
                dve.tensor_reduce(negm[:, qt % NP:qt % NP + 1], s_ps[:, qt % 2, 0:n], AX.X, ALU.max,
                                  negate=True).then_inc(max_done, 1)

            def invert(hb, qt):
                u = hb * NQ + qt
                dve.wait_ge(exp_done, u + 1)
                if at_least(u, NP):
                    dve.wait_ge(p_done, u - NP + 1)
                dve.reciprocal(rinv[:, qt % NP:qt % NP + 1], rsum[:, qt % NP:qt % NP + 1]).then_inc(inv_done, 1)

            def keep_lo(hb, qt):
                for k0, count, n in batches(qt):
                    dve.wait_ge(th_done, hb * NB + (n + 1))
                    c, q0 = qt // CQ, (qt % CQ) * P
                    dve.tensor_tensor(ptl[c][:, k0:k0 + count, q0:q0 + P],
                                      t_ps[:, n % 2, 0:count * P].rearrange("p (k q) -> p k q", q=P),
                                      pth[c][:, k0:k0 + count, q0:q0 + P].bitcast(F32), ALU.subtract).then_inc(tl_done, 1)

            def task(b, t, k, hi, bank):
                src = r_ps[:, bank, :]
                if t[0] == "o":
                    dve.wait_ge(task_done, k + 1)
                    ob = 1 - b if t[2] else b
                    y = yT[:, t[3], ob * S + t[1] * CH:ob * S + (t[1] + 1) * CH]
                    if at_least(k, NTASK):
                        dve.wait_ge(task_out, k - NTASK + 1)
                    dve.tensor_tensor(y, y, src, ALU.add).then_inc(task_out, 1)
                    return
                if t[0] == "vt":
                    dve.wait_ge(task_done, k + 1)
                    dve.tensor_copy(vt[:, t[1], :], src).then_inc(task_out, 1)
                    return
                dve.wait_ge(task_hi, hi + 1)
                h, l = pair_of(t, b)
                if t[0] == "q":
                    dve.scalar_tensor_tensor(out=l, in0=src, scalar=SCALE, in1=h.bitcast(F32), op0=ALU.mult,
                                             op1=ALU.subtract).then_inc(task_out, 1)
                else:
                    dve.tensor_tensor(l, src, h.bitcast(F32), ALU.subtract).then_inc(task_out, 1)

            def half(hb, h, b, first, last):
                (k, hi), n, m = bases(hb), 0, 0
                for qt, tasks in enumerate(plan(first, last)):
                    if qt < NQ - 1:
                        invert(hb, qt + 1)
                    elif not last:
                        invert(hb + 1, 0)
                    if qt < NQ - 2:
                        maximum(hb, qt + 2)
                    elif not last:
                        maximum(hb + 1, qt + 2 - NQ)
                    keep_lo(hb, qt)
                    for t in tasks:
                        task(b, t, k + n, hi + m, bank_of(b, first, n))
                        m += t[0] not in WHOLE
                        n += 1

            def begin():
                for n, t in enumerate(PRE):
                    task(1, t, n, sum(p[0] not in WHOLE for p in PRE[:n]), n % 2)
                for qt in range(2):
                    maximum(0, qt)
                invert(0, 0)

            def end():
                k = bases(HB - 1)[0] + sum(len(u) for u in plan(False, True))
                hi = bases(HB - 1)[1] + sum(t[0] not in WHOLE for u in plan(False, True) for t in u)
                for n, t in enumerate([("pv", 1, True), ("o", 1, True, 0), ("o", 1, True, 1)]):
                    task(0, t, k + n, hi, (k + n) % 2)

            walk(dve, half, begin, end)


def prepare(nc, tag, xT, xh, xl, yT, ident):
    with Phase(nc, tag) as ph:
        y_in = [ph.sem(f"y_in{c}") for c in range(T // CH)]
        cleared = ph.sem("cleared")
        ident_done = ph.sem("ident_done")
        hi_done = ph.sem("hi_done")
        lo_done = ph.sem("lo_done")
        block = ph.block()

        @block.sync
        def _(sp):
            for c in range(T // CH):
                t = slice(c * CH, (c + 1) * CH)
                sp.dma_start(yT[:, :, t], xT[:, :, t]).then_inc(y_in[c], 16)

        @block.gpsimd
        def _(pool):
            pool.memset(ident[:], 0.0).then_inc(cleared, 1)
            pool.wait_ge(cleared, 1)
            pool.affine_select(out=ident[:], in_=ident[:], compare_op=ALU.not_equal, fill=1.0, base=0,
                               pattern=[[-1, P]], channel_multiplier=1).then_inc(ident_done, 1)
            pool.wait_ge(ident_done, 1)

        @block.scalar
        def _(act):
            for c in range(T // CH):
                t = slice(c * CH, (c + 1) * CH)
                act.wait_ge(y_in[c], 16)
                act.activation(xh[:, :, t], yT[:, :, t], ACT.Copy).then_inc(hi_done, 1)

        @block.vector
        def _(dve):
            for c in range(T // CH):
                t = slice(c * CH, (c + 1) * CH)
                dve.wait_ge(hi_done, c + 1)
                dve.tensor_tensor(xl[:, :, t], yT[:, :, t], xh[:, :, t].bitcast(F32), ALU.subtract).then_inc(lo_done, 1)
            dve.wait_ge(lo_done, T // CH)


def program(nc, a, out):
    with ExitStack() as stack:
        def sb(name, shape, dt=F32):
            return stack.enter_context(nc.sbuf_tensor(name, shape, dt))

        xh = sb("xh", [P, DT, T], F32R)
        xl = sb("xl", [P, DT, T], F32R)
        yT = sb("yT", [P, DT, T])
        ident = sb("ident", [P, P])
        psum = stack.enter_context(nc.psum_tensor("psum", [P, 8, CH], F32))
        rows = out.rearrange("b s d -> (b s) d")
        norm_sems = layer_norm_semaphores(nc, stack)
        prepare(nc, "in", a["xT"], xh, xl, yT, ident)

        causal_attention(nc, "a0", a, xh, xl, yT, ident, psum)
        layer_norm(nc, "n0", 0, norm_sems, yT, xh, xl, ident, psum)

        w = {"groups": 1, "shared_tiles": NSH0, "topk": 2, "gate_w": a["gw0"], "gate_b": None, "sel": a["sel0"],
             "gu": a["gu0"], "bias": a["bias0"], "down": a["down0"]}
        mixture(nc, "f0", w, xh, xl, yT, ident, psum, True)
        layer_norm(nc, "n1", 1, norm_sems, yT, xh, xl, ident, psum)

        grouped_attention(nc, "a1", a, xh, xl, yT, ident, psum)
        layer_norm(nc, "n2", 2, norm_sems, yT, xh, xl, ident, psum)

        w = {"groups": 2, "shared_tiles": NSH1, "topk": 6, "gate_w": a["gw1"], "gate_b": a["gb1"], "sel": a["sel1"],
             "gu": a["gu1"], "bias": a["bias1"], "down": a["down1"], "b2": a["b21"]}
        mixture(nc, "f1", w, xh, xl, yT, ident, psum, False)
        layer_norm(nc, "n3", 3, norm_sems, yT, xh, xl, ident, psum, rows)


def by_tiles(w, groups, shared, nsh):
    n = w.shape[2]
    e = w.reshape(groups, NE, NJ, SLICE, n).transpose(0, 2, 1, 3, 4).reshape(groups * NJ, P, n)
    s = np.zeros((nsh * P, n), w.dtype)
    s[:shared.shape[0]] = shared
    return np.concatenate([e, s.reshape(nsh, P, n)])


def by_inputs(t):
    return t.reshape(t.shape[0], P, DT, P).transpose(0, 3, 2, 1)


def pack_ffn(gate, up, down, sgate, sup, sdown, groups, nsh, b_gate=None, b_up=None, sb_gate=None, sb_up=None):
    nt = groups * NJ + nsh
    g = by_inputs(by_tiles(gate, groups, sgate, nsh)).reshape(nt, P, DT * P)
    u = by_inputs(by_tiles(up, groups, sup, nsh)).reshape(nt, P, DT * P)
    if b_gate is None:
        bias = np.zeros((nt, P, 2), gate.dtype)
    else:
        bias = np.concatenate([by_tiles(b_gate[:, :, None], groups, sb_gate[:, None], nsh),
                               by_tiles(b_up[:, :, None], groups, sb_up[:, None], nsh)], axis=2)
    return np.concatenate([g, u], axis=2), bias.transpose(1, 0, 2), by_tiles(down, groups, sdown, nsh)


def selectors(groups, gate):
    ne = NE * groups
    sel = np.zeros((ne + 1, groups + (1 if gate else 0), P), np.float32)
    for e in range(ne):
        sel[e, e // NE, (e % NE) * SLICE:(e % NE + 1) * SLICE] = 1
    if gate:
        sel[ne, groups, :] = 1
    return sel


def inner(m):
    return m.reshape(DT, P, m.shape[1]).transpose(1, 0, 2)


def layouts(i):
    i = {k: np.asarray(v) for k, v in i.items()}
    a = {"xT": inner(i["L0_attn_x"].reshape(T, D).T)}
    a["qkv0"] = np.stack([w.transpose(0, 2, 1).reshape(H0, DT, P, E0).transpose(0, 2, 1, 3)
                          for w in (i["L0_attn_W_Q"], i["L0_attn_W_K"], i["L0_attn_W_V"])], axis=2)
    a["o0"] = i["L0_attn_W_O"].transpose(0, 2, 1)
    a["gu0"], a["bias0"], a["down0"] = pack_ffn(i["L0_ffn_w_gate"].transpose(0, 2, 1), i["L0_ffn_w_up"].transpose(0, 2, 1),
                                    i["L0_ffn_w_down"], i["L0_ffn_sw_gate"].T, i["L0_ffn_sw_up"].T,
                                    i["L0_ffn_sw_down"], 1, NSH0)
    pad = np.zeros((1, D), np.float32)
    a["gw0"] = inner(np.concatenate([i["L0_ffn_gate_w"], i["L0_ffn_shared_gate_w"].T, pad]).T)
    a["sel0"] = selectors(1, True)
    a["gu1"], a["bias1"], a["down1"] = pack_ffn(i["L1_ffn_w1"], i["L1_ffn_w3"], i["L1_ffn_w2"].transpose(0, 2, 1),
                                    i["L1_ffn_ws1"], i["L1_ffn_ws3"], i["L1_ffn_ws2"].T, 2, NSH1,
                                    i["L1_ffn_b1"], i["L1_ffn_b3"], i["L1_ffn_bs1"], i["L1_ffn_bs3"])
    a["gw1"] = inner(i["L1_ffn_gate_w"].T)
    a["gb1"] = np.broadcast_to(i["L1_ffn_gate_b"], (P, 2 * NE))
    a["b21"] = np.concatenate([i["L1_ffn_b2"], i["L1_ffn_bs2"][None]])
    a["sel1"] = selectors(2, False)
    a["wqkv1"] = inner(i["L1_attn_Wqkv"])
    a["bqkv1"] = i["L1_attn_bqkv"].reshape(3, P).T
    a["wo1"] = inner(i["L1_attn_Wout"])
    a["bo1"] = i["L1_attn_bout"].reshape(DT, P).T
    return {k: np.ascontiguousarray(v) for k, v in a.items()}


def kernel(**inputs):
    import concourse.bacc as _bacc
    from concourse.bass_utils import run_bass_kernel_spmd as _run

    nc = _bacc.Bacc("TRN2", target_bir_lowering=False, num_devices=1)
    arrays, aps = {}, {}
    for name, v in layouts(inputs).items():
        arrays[f"in_{name}"] = v
        aps[name] = nc.dram_tensor(f"in_{name}", v.shape, mybir.dt.from_np(v.dtype), kind="ExternalInput").ap()
    out = nc.dram_tensor("out", (B, S, D), F32, kind="ExternalOutput").ap()
    program(nc, aps, out)
    return _run(nc, [arrays], core_ids=[0]).results[0]["out"]
```
